# Optimizing a Trainium2 kernel written in Bass

```python
import numpy as np
import jax
import jax.numpy as jnp

def _softmax(x, axis=-1):
    return jax.nn.softmax(x, axis=axis)

def _gelu(x):
    return jax.nn.gelu(x, approximate=True)

def _silu(x):
    return jax.nn.silu(x)

def _sigmoid(x):
    return jax.nn.sigmoid(x)

def _layernorm(x, axis=-1, eps=1e-05):
    m = jnp.mean(x, axis=axis, keepdims=True)
    v = jnp.var(x, axis=axis, keepdims=True)
    return (x - m) / jnp.sqrt(v + eps)

def _scatter_add(tgt, idx, src, axis=0):
    return tgt.at[idx].add(src)

def _segment_sum(src, seg, n):
    return jax.ops.segment_sum(src, seg, n)
kernel_name = 'mk_decoder_preln_d1_seqx_r4_874529'

def setup_inputs(seed: int=0):
    np.random.seed(seed)
    _w = jnp.asarray

    def _rec_inputs():
        import jax
        import jax.numpy as jnp
        _rk = jax.random.key(seed)
        x = 7.22e-05 + 1 * jax.random.normal(jax.random.fold_in(_rk, 1), (2, 1024, 256), jnp.float32)
        _lenS = 1024 - jax.random.randint(jax.random.fold_in(_rk, 7), (2,), 0, max(1, 1024 // 4) + 1, jnp.int32)
        _lenS2 = 77 - jax.random.randint(jax.random.fold_in(_rk, 8), (2,), 0, max(1, 77 // 4) + 1, jnp.int32)
        _ctx_1024P = jax.random.normal(jax.random.fold_in(_rk, 11), (2, 16, 256), jnp.float32)
        _ctx_1024c = jax.random.dirichlet(jax.random.fold_in(_rk, 511), 0.3 * jnp.ones((16,), jnp.float32), (2, 77))
        _ctx_1024t = jnp.einsum('bsk,bkd->bsd', _ctx_1024c, _ctx_1024P)
        _ctx_1024t = _ctx_1024t * jax.lax.rsqrt(jnp.mean(jnp.square(_ctx_1024t)) + 1e-12) * 0.953939
        ctx_1024 = 4.13588e-05 + 0.999923 * (_ctx_1024t + 0.3 * jax.random.normal(jax.random.fold_in(_rk, 611), (2, 77, 256), jnp.float32))
        return (x, ctx_1024)
    x, ctx_1024 = _rec_inputs()

    def _L0_attn_setup():
        import jax, jax.numpy as jnp
        import numpy as np
        DIM = 256
        HEADS = 16
        DIM_HEAD = 64
        SCALE = 16.0
        EPS = 1e-05

        def layernorm(x, g):
            mean = jnp.mean(x, axis=-1, keepdims=True)
            var = jnp.var(x, axis=-1, keepdims=True)
            return (x - mean) * jax.lax.rsqrt(var + EPS) * g

        def l2norm(t):
            return t / jnp.maximum(jnp.linalg.norm(t, axis=-1, keepdims=True), 1e-12)
        key = jax.random.key(seed)
        ks = jax.random.split(key, 5)
        inner = HEADS * DIM_HEAD
        x = jax.random.normal(ks[0], (2, 512, DIM), dtype=jnp.float32)
        Wq = jax.random.normal(ks[1], (inner, DIM), dtype=jnp.float32) * 0.02
        Wkv = jax.random.normal(ks[2], (2 * DIM_HEAD, DIM), dtype=jnp.float32) * 0.02
        Wout = jax.random.normal(ks[3], (DIM, inner), dtype=jnp.float32) * 0.02
        g1 = jnp.ones((DIM,), dtype=jnp.float32)
        g2 = jnp.ones((DIM,), dtype=jnp.float32)
        return {'x': x, 'g1': g1, 'Wq': Wq, 'Wkv': Wkv, 'Wout': Wout, 'g2': g2}
    _L0_attn_all = _L0_attn_setup()
    _L0_attn_in = {k: v for k, v in _L0_attn_all.items() if k in ('g1', 'Wq', 'Wkv', 'Wout', 'g2')}
    del _L0_attn_all

    def _L0_xattn_setup():
        import jax, jax.numpy as jnp
        import numpy as np
        D_MODEL = 256
        NUM_HEADS = 16
        D_K = D_MODEL // NUM_HEADS

        def _split_heads(x):
            B, S, D = x.shape
            return x.reshape(B, S, NUM_HEADS, D_K).transpose(0, 2, 1, 3)
        key = jax.random.key(seed)
        ks = jax.random.split(key, 11)
        B, S, D = (4, 512, D_MODEL)
        scale = 1.0 / np.sqrt(D)
        inp = {'query': jax.random.normal(ks[0], (B, S, D), jnp.float32), 'key': jax.random.normal(ks[1], (B, S, D), jnp.float32), 'value': jax.random.normal(ks[2], (B, S, D), jnp.float32), 'W_q': jax.random.normal(ks[3], (D, D), jnp.float32) * scale, 'b_q': jax.random.normal(ks[4], (D,), jnp.float32) * scale, 'W_k': jax.random.normal(ks[5], (D, D), jnp.float32) * scale, 'b_k': jax.random.normal(ks[6], (D,), jnp.float32) * scale, 'W_v': jax.random.normal(ks[7], (D, D), jnp.float32) * scale, 'b_v': jax.random.normal(ks[8], (D,), jnp.float32) * scale, 'W_out': jax.random.normal(ks[9], (D, D), jnp.float32) * scale, 'b_out': jax.random.normal(ks[10], (D,), jnp.float32) * scale}
        return inp
    _L0_xattn_all = _L0_xattn_setup()
    _L0_xattn_in = {k: v for k, v in _L0_xattn_all.items() if k in ('W_q', 'b_q', 'W_k', 'b_k', 'W_v', 'b_v', 'W_out', 'b_out')}
    del _L0_xattn_all

    def _L0_ffn_setup():
        import jax, jax.numpy as jnp
        import numpy as np
        B, S, D = (2, 512, 256)
        E = 4
        H = 4 * D
        key = jax.random.key(seed)
        k_x, k_r, k_wv, k_wp = jax.random.split(key, 4)
        x = jax.random.normal(k_x, (B, S, D), dtype=jnp.float32)
        w_router = jax.random.normal(k_r, (D, E), dtype=jnp.float32) * 0.02
        w_v = jax.random.normal(k_wv, (E, D, 2 * H), dtype=jnp.float32) * 0.02
        w_proj = jax.random.normal(k_wp, (E, H, D), dtype=jnp.float32) * 0.02
        return {'x': x, 'w_router': w_router, 'w_v': w_v, 'w_proj': w_proj}
    _L0_ffn_all = _L0_ffn_setup()
    _L0_ffn_in = {k: v for k, v in _L0_ffn_all.items() if k in ('w_router', 'w_v', 'w_proj')}
    del _L0_ffn_all
    return {'x': x, 'ctx_1024': ctx_1024, 'L0_attn_g1': _L0_attn_in['g1'], 'L0_attn_Wq': _L0_attn_in['Wq'], 'L0_attn_Wkv': _L0_attn_in['Wkv'], 'L0_attn_Wout': _L0_attn_in['Wout'], 'L0_attn_g2': _L0_attn_in['g2'], 'L0_xattn_W_q': _L0_xattn_in['W_q'], 'L0_xattn_b_q': _L0_xattn_in['b_q'], 'L0_xattn_W_k': _L0_xattn_in['W_k'], 'L0_xattn_b_k': _L0_xattn_in['b_k'], 'L0_xattn_W_v': _L0_xattn_in['W_v'], 'L0_xattn_b_v': _L0_xattn_in['b_v'], 'L0_xattn_W_out': _L0_xattn_in['W_out'], 'L0_xattn_b_out': _L0_xattn_in['b_out'], 'L0_ffn_w_router': _L0_ffn_in['w_router'], 'L0_ffn_w_v': _L0_ffn_in['w_v'], 'L0_ffn_w_proj': _L0_ffn_in['w_proj']}

def reference(x, ctx_1024, L0_attn_g1, L0_attn_Wq, L0_attn_Wkv, L0_attn_Wout, L0_attn_g2, L0_xattn_W_q, L0_xattn_b_q, L0_xattn_W_k, L0_xattn_b_k, L0_xattn_W_v, L0_xattn_b_v, L0_xattn_W_out, L0_xattn_b_out, L0_ffn_w_router, L0_ffn_w_v, L0_ffn_w_proj):
    import jax
    import jax.numpy as jnp

    def _L0_attn_ref(x, g1, Wq, Wkv, Wout, g2):
        import jax, jax.numpy as jnp
        import numpy as np
        DIM = 256
        HEADS = 16
        DIM_HEAD = 64
        SCALE = 16.0
        EPS = 1e-05

        def layernorm(x, g):
            mean = jnp.mean(x, axis=-1, keepdims=True)
            var = jnp.var(x, axis=-1, keepdims=True)
            return (x - mean) * jax.lax.rsqrt(var + EPS) * g

        def l2norm(t):
            return t / jnp.maximum(jnp.linalg.norm(t, axis=-1, keepdims=True), 1e-12)
        b, n, _ = x.shape
        xn = layernorm(x, g1)
        q = xn @ Wq.T
        kv = xn @ Wkv.T
        k, v = (kv[..., :DIM_HEAD], kv[..., DIM_HEAD:])
        q = q.reshape(b, n, HEADS, DIM_HEAD).transpose(0, 2, 1, 3)
        q = q * SCALE
        q, k = (l2norm(q), l2norm(k))
        srt = np.sqrt(SCALE).astype(np.float32)
        q, k = (q * srt, k * srt)
        sim = jnp.einsum('bhid,bjd->bhij', q, k)
        max_neg = -jnp.finfo(sim.dtype).max
        causal_mask = jnp.triu(jnp.ones((n, n), dtype=bool), 1)
        sim = jnp.where(causal_mask, max_neg, sim)
        attn = jax.nn.softmax(sim.astype(jnp.float32), axis=-1).astype(sim.dtype)
        out = jnp.einsum('bhij,bjd->bhid', attn, v)
        out = out.transpose(0, 2, 1, 3).reshape(b, n, HEADS * DIM_HEAD)
        out = out @ Wout.T
        return layernorm(out, g2)

    def _L0_xattn_ref(query, key, value, W_q, b_q, W_k, b_k, W_v, b_v, W_out, b_out):
        import jax, jax.numpy as jnp
        import numpy as np
        D_MODEL = 256
        NUM_HEADS = 16
        D_K = D_MODEL // NUM_HEADS

        def _split_heads(x):
            B, S, D = x.shape
            return x.reshape(B, S, NUM_HEADS, D_K).transpose(0, 2, 1, 3)
        q = _split_heads(query @ W_q.T + b_q)
        k = _split_heads(key @ W_k.T + b_k)
        v = _split_heads(value @ W_v.T + b_v)
        scores = jnp.einsum('bhqd,bhkd->bhqk', q, k) / jnp.sqrt(jnp.float32(D_K))
        probs = jax.nn.softmax(scores, axis=-1)
        out = jnp.einsum('bhqk,bhkd->bhqd', probs, v)
        B, H, S, dk = out.shape
        out = out.transpose(0, 2, 1, 3).reshape(B, S, H * dk)
        return out @ W_out.T + b_out

    def _L0_ffn_ref(x, w_router, w_v, w_proj):
        import jax, jax.numpy as jnp
        import numpy as np
        B, S, D = (2, 512, 256)
        E = 4
        H = 4 * D
        logits = jnp.einsum('bsd,de->bse', x, w_router)
        probs = jax.nn.softmax(logits, axis=-1)
        expert_idx = jnp.argmax(probs, axis=-1)
        gv = jnp.einsum('bsd,edh->ebsh', x, w_v)
        gate_raw, value = jnp.split(gv, 2, axis=-1)
        h = gate_raw * jax.nn.sigmoid(gate_raw) * value
        y = jnp.einsum('ebsh,ehd->ebsd', h, w_proj)
        onehot = jax.nn.one_hot(expert_idx, w_v.shape[0], dtype=x.dtype)
        return jnp.einsum('bse,ebsd->bsd', onehot, y)
    x = x + _L0_attn_ref(_layernorm(x, axis=-1), L0_attn_g1, L0_attn_Wq, L0_attn_Wkv, L0_attn_Wout, L0_attn_g2)
    x = x + _L0_xattn_ref(_layernorm(x, axis=-1), ctx_1024, ctx_1024, L0_xattn_W_q, L0_xattn_b_q, L0_xattn_W_k, L0_xattn_b_k, L0_xattn_W_v, L0_xattn_b_v, L0_xattn_W_out, L0_xattn_b_out)
    x = x + _L0_ffn_ref(_layernorm(x, axis=-1), L0_ffn_w_router, L0_ffn_w_v, L0_ffn_w_proj)
    return x

_drawn_inputs = setup_inputs


def setup_inputs(seed=0):
    import zlib

    import numpy as np

    out = dict(_drawn_inputs(seed))
    spreads = {'L0_attn_g1': (1.0, 0.2), 'L0_attn_g2': (1.0, 0.2)}
    factors = {'L0_xattn_b_q': 5.434, 'L0_xattn_b_k': 8.0, 'L0_ffn_w_router': 2.948}
    for name, (base, spread) in spreads.items():
        noise = np.random.default_rng([zlib.crc32(name.encode()), seed]).standard_normal(out[name].shape)
        drawn = base * np.exp(spread * noise) if base else spread * noise
        out[name] = jnp.asarray(drawn.astype(out[name].dtype))
    for name, factor in factors.items():
        out[name] = (out[name] * factor).astype(out[name].dtype)
    return out
```

```python
from contextlib import ExitStack

import concourse.bass as bass
from concourse import mybir

F32 = mybir.dt.float32
F32R = mybir.dt.float32r
I32 = mybir.dt.int32
ACT = mybir.ActivationFunctionType
ALU = mybir.AluOpType
AX = mybir.AxisListType

P = 128
BATCH, SEQ, DIM = 2, 1024, 256
TOKENS = BATCH * SEQ
TILES = TOKENS // P
TPB = SEQ // P
CH = DIM // P
HEADS, DH = 16, 64
GROUPS = 4
HPG = HEADS // GROUPS
QKV = HEADS * DH + 2 * DH
NQ = 3
QB = QKV // NQ
HPB = QB // DH
CTX, CPAD = 77, 80
XH, XD = 16, 16
HK = XH * CPAD
HKC = HK // P
SB = 4 * CPAD
EXP, HID = 4, 1024
SORTED = TOKENS // P + EXP - 1
ROW = DIM + 1
EPS = 1e-5
SIM_SCALE = 16.0
NEG = -1e30
RING = 3
KV = TPB + 2
WB = 4

GAPS = [
    [("xattn_out", -3, 0), ("heads_out", -1, 3), ("z2_turn", -2, 0), ("q_turn", 1, 0), ("norm_x", 2, 0)],
    [("heads_out", 0, 0), ("out_turn", -1, 0), ("z_turn", 2, 0), ("scores", -2, 0)],
    [("heads_out", 0, 1), ("out_proj", -1, 0), ("qkv", 2, 0)],
    [("heads_out", 0, 2), ("probs_turn", -2, 0)],
]
JOBS = {
    "norm_x": [],
    "z_turn": ["act"],
    "qkv": ["dve"] * NQ,
    "q_turn": ["act", "dve", "act", "dve", "act"],
    "heads_out": ["dve"],
    "out_turn": ["act", "act"],
    "out_proj": ["dve"],
    "z2_turn": ["act"],
    "scores": ["dve"] * 4,
    "probs_turn": ["act", "act", "act"],
    "xattn_out": ["dve"],
}
FIRST_SLOT, LAST_SLOT = -2, TILES - 1 + 3


def plan_steps():
    steps, start = [], []
    for t in range(TILES):
        for g in range(GROUPS):
            start.append(len(steps))
            steps += [(t, g, j) for j in range(t % TPB + 1)]
    start.append(len(steps))
    return steps, start


def plan_side(first_job, freed):
    gaps, job = {}, first_job
    for slot in range(FIRST_SLOT, LAST_SLOT + 1):
        for gap in range(GROUPS):
            here = []
            for name, shift, extra in GAPS[gap]:
                t = slot + shift
                if 0 <= t < TILES:
                    here.append((name, t, extra, job))
                    for engine in JOBS[name]:
                        n = 1 + sum(1 for e, _ in freed if e == engine)
                        freed.append((engine, n))
                        job += 1
            gaps[slot, gap] = here
    return gaps


def build(nc, x, wqkv_t, wout_t, g1, g2, ctx_t, xwq, xwk_t, xwv_t, xwout_t, biases, xbout,
          wr_t, w_v, w_proj, out):
    steps, group_start = plan_steps()
    N_STEPS = len(steps)
    setup = [("kv", m) for m in range(4)]
    for b in range(BATCH):
        setup += [("g", b, c, n) for c in range(CH) for n in range(4)]
        setup += [("bias", b, n) for n in range(4)]
        setup += [("v", b, n) for n in range(HKC)]
    freed = []
    for s in setup:
        e = "dve" if s[0] == "kv" else "act"
        freed.append((e, 1 + sum(1 for q, _ in freed if q == e)))
    side = plan_side(len(setup), freed)
    N_SIDE = len(freed)

    x_rows = x.rearrange("(t p) d -> p t d", p=P)

    with ExitStack() as keep:
        def sem(name):
            return keep.enter_context(nc.semaphore(name))

        def sb(ctx, name, shape, dt=F32):
            return ctx.enter_context(nc.sbuf_tensor(name, shape, dt))

        xall = sb(keep, "xall", [P, TILES, ROW])
        ident = sb(keep, "ident", [P, P])
        half = sb(keep, "half", [P, HEADS + 2])
        logits = sb(keep, "logits", [P, TILES, EXP])
        pos_i = sb(keep, "pos_i", [P, TILES], I32)
        expert_i = sb(keep, "expert_i", [P, SORTED + 1], I32)
        tri = sb(keep, "tri", [P, P])
        ones = sb(keep, "ones", [P, P])
        pad_row = sb(keep, "pad_row", [P, ROW])
        idnum = sb(keep, "idnum", [P, TILES], I32)

        early = ExitStack()
        wqkv = sb(early, "wqkv", [P, CH, QKV])
        wout = sb(early, "wout", [P, HEADS * DH // P, DIM])
        g1c = sb(early, "g1c", [P, CH])
        g2b = sb(early, "g2b", [P, DIM])
        boutb = sb(early, "boutb", [P, DIM])
        wrb = sb(early, "wrb", [P, EXP, DIM])
        G = [sb(early, f"G{b}", [P, CH, HK]) for b in range(BATCH)]
        BI = [sb(early, f"BI{b}", [P, HK], F32R) for b in range(BATCH)]
        VP = [sb(early, f"VP{b}", [P, HKC, DIM]) for b in range(BATCH)]
        pick = sb(early, "pick", [P, P], F32R)
        stat = sb(early, "stat", [P, TILES, 6])
        mv = sb(early, "mv", [P, TILES, 2])
        rin = sb(early, "rin", [P, TILES])
        rstd = sb(early, "rstd", [P, TILES])
        floor = sb(early, "floor", [P, HEADS + 2])
        rn = sb(early, "rn", [P, HEADS + 2])
        temp = ExitStack()
        wk = sb(temp, "wk", [P, CH, DIM])
        wv = sb(temp, "wv", [P, CH, DIM])
        wq2 = sb(temp, "wq2", [P, CH, DIM])
        wo2 = sb(temp, "wo2", [P, CH, DIM])
        ctxs = sb(temp, "ctxs", [P, CH, BATCH * CTX])
        bcol = sb(temp, "bcol", [P, 3, CH])
        bqb = sb(temp, "bqb", [P, CH, P])
        kvT = sb(temp, "kvT", [P, 4, BATCH, CPAD])
        own = sb(temp, "own", [P, 8, CPAD])
        kbd = sb(temp, "kbd", [P, CH, 8, CPAD])
        vbd = sb(temp, "vbd", [P, CH, 8, CPAD])
        braw = sb(temp, "braw", [P, HK])
        bhi = sb(temp, "bhi", [P, HK], F32R)
        blo = sb(temp, "blo", [P, HK])
        rowm = sb(temp, "rowm", [P, 2])
        temp.close()
        z = [sb(early, f"z{n}", [P, DIM]) for n in range(2)]
        zT = sb(early, "zT", [P, CH, P])
        sq = sb(early, "sq", [P, NQ, QB])
        ss = sb(early, "ss", [P, HEADS + 2])
        ssc = sb(early, "ssc", [P, HEADS + 2])
        qn = sb(early, "qn", [P, HEADS + 2, DH])
        qhl = sb(early, "qhl", [P, HEADS + 2, 2, DH], F32R)
        kdup = sb(early, "kdup", [P, 2, 2, DH])
        qT = [sb(early, f"qT{n}", [P, HEADS, P], F32R) for n in range(2)]
        kT = sb(early, "kT", [P, KV, 2, P], F32R)
        vhi = sb(early, "vhi", [P, KV, DH + 2], F32R)
        vlo = sb(early, "vlo", [P, KV, DH + 2], F32R)
        pr = sb(early, "pr", [P, RING, HPG * P])
        ph = sb(early, "ph", [P, RING, HPG * P], F32R)
        pl = sb(early, "pl", [P, RING, HPG * P], F32R)
        oT = sb(early, "oT", [P, 2, HPG * P])
        rl = sb(early, "rl", [P, HPG])
        on = [sb(early, f"on{n}", [P, HEADS * DH]) for n in range(2)]
        onT = sb(early, "onT", [P, HEADS * DH // P, P])
        st2 = sb(early, "st2", [P, 6])
        mv2 = sb(early, "mv2", [P, 2])
        ri2 = sb(early, "ri2", [P, 1])
        rs2 = sb(early, "rs2", [P, 1])
        xa = sb(early, "xa", [P, DIM])
        z2 = sb(early, "z2", [P, DIM])
        z2T = sb(early, "z2T", [P, CH, P])
        mx = sb(early, "mx", [P, XH])
        sc = sb(early, "sc", [P, XH, CPAD])
        sm = sb(early, "sm", [P, XH])
        rsm = sb(early, "rsm", [P, XH])
        pT = sb(early, "pT", [P, HKC, P])
        z3 = sb(early, "z3", [P, DIM])
        junk = sb(early, "junk", [P, DIM])
        early.close()

        late = ExitStack()
        wvs = sb(late, "wvs", [P, EXP, CH, 2 * HID])
        wps = sb(late, "wps", [P, EXP, HID // P, DIM])
        xs = sb(late, "xs", [P, 3, ROW])
        fst = sb(late, "fst", [P, 6])
        fmv = sb(late, "fmv", [P, 2])
        fri = sb(late, "fri", [P, 1])
        frs = sb(late, "frs", [P, 1])
        fz = sb(late, "fz", [P, DIM])
        fzT = sb(late, "fzT", [P, CH, P])
        gate = sb(late, "gate", [P, 2, HID])
        hh = sb(late, "hh", [P, 2, HID])
        hT = sb(late, "hT", [P, HID // P, P])
        res = sb(late, "res", [P, 2, DIM])
        best = sb(late, "best", [P, TILES])
        eq = sb(late, "eq", [P, TILES, EXP])
        oh = sb(late, "oh", [P, TILES, EXP])
        left = sb(late, "left", [P, TILES])
        base = sb(late, "base", [P, TILES + 1, EXP])
        tot = sb(late, "tot", [P, TILES, EXP])
        cnt_i = sb(late, "cnt_i", [P, EXP], I32)
        cnt_s = sb(late, "cnt_s", [P, EXP], I32)
        cnt_f = sb(late, "cnt_f", [P, EXP])
        end = sb(late, "end", [P, EXP + 1])
        off = sb(late, "off", [P, EXP])
        rank = sb(late, "rank", [P, TILES, EXP])
        posf = sb(late, "posf", [P, TILES])
        tnum_i = sb(late, "tnum_i", [P, SORTED + 1], I32)
        tnum = sb(late, "tnum", [P, SORTED + 1])
        ecmp = sb(late, "ecmp", [P, SORTED + 1])
        late.close()

        S = [keep.enter_context(nc.psum_tensor(f"S{n}", [P, 512], F32)) for n in range(2)]
        O = [keep.enter_context(nc.psum_tensor(f"O{n}", [P, 512], F32)) for n in range(2)]
        W = [keep.enter_context(nc.psum_tensor(f"W{n}", [P, 512], F32)) for n in range(WB)]

        sorted_rows = nc.dram_tensor("sorted_rows", [SORTED * P, ROW], F32, kind="Internal").ap()

        x_in = [sem(f"x_in{b}") for b in range(BATCH)]
        w_in = sem("w_in")
        wk_in = sem("wk_in")
        wo_in = sem("wo_in")
        rows_in = sem("rows_in")
        consts = sem("consts")
        spread = sem("spread")
        dconst = sem("dconst")
        wq_scaled = sem("wq_scaled")
        side_ready = sem("side_ready")
        act_freed = sem("act_freed")
        dve_freed = sem("dve_freed")
        own_ok = sem("own_ok")
        bd_ready = sem("bd_ready")
        bd_used = sem("bd_used")
        braw_ready = sem("braw_ready")
        bias_step = sem("bias_step")
        stats_ok = sem("stats_ok")
        stats_in = sem("stats_in")
        rstd_ok = sem("rstd_ok")
        z_ready = sem("z_ready")
        sq_ready = sem("sq_ready")
        ss_ready = sem("ss_ready")
        ssc_ready = sem("ssc_ready")
        rn_ready = sem("rn_ready")
        qhi_ready = sem("qhi_ready")
        qlo_ready = sem("qlo_ready")
        kdup_ready = sem("kdup_ready")
        v_ready = sem("v_ready")
        s_ready = sem("s_ready")
        p_ready = sem("p_ready")
        masked = sem("masked")
        ph_ready = sem("ph_ready")
        pl_ready = sem("pl_ready")
        pv_done = sem("pv_done")
        ot_ready = sem("ot_ready")
        rl_ready = sem("rl_ready")
        on_ready = sem("on_ready")
        ln_step = sem("ln_step")
        ln_root = sem("ln_root")
        ln_self = sem("ln_self")
        xa_ready = sem("xa_ready")
        x1_ready = sem("x1_ready")
        xa_step = sem("xa_step")
        z2_ready = sem("z2_ready")
        x1b_ready = sem("x1b_ready")
        mx_ready = sem("mx_ready")
        sc_ready = sem("sc_ready")
        pe_ready = sem("pe_ready")
        sm_ready = sem("sm_ready")
        rsm_ready = sem("rsm_ready")
        pn_ready = sem("pn_ready")
        x2_ready = sem("x2_ready")
        z3_ready = sem("z3_ready")
        logit_ready = sem("logit_ready")
        act_done = sem("act_done")
        pe_done = sem("pe_done")
        route = sem("route")
        counted = sem("counted")
        pos_ready = sem("pos_ready")
        pad_out = sem("pad_out")
        scattered = sem("scattered")
        ffn_w = sem("ffn_w")
        tile_num = sem("tile_num")
        xs_in = [sem(f"xs_in{n}") for n in range(3)]
        f_self = sem("f_self")
        f_root = sem("f_root")
        f_step = sem("f_step")
        fz_ready = sem("fz_ready")
        f_turn = sem("f_turn")
        fzT_ready = sem("fzT_ready")
        up_ready = sem("up_ready")
        gate_ready = sem("gate_ready")
        h_ready = sem("h_ready")
        h_turned = sem("h_turned")
        hT_ready = sem("hT_ready")
        down_ready = sem("down_ready")
        res_ready = sem("res_ready")
        stored = [sem(f"stored{n}") for n in range(2)]

        block = keep.enter_context(nc.Block())

        def freed_wait(eng, job):
            if job >= WB:
                who, n = freed[job - WB]
                eng.wait_ge(act_freed if who == "act" else dve_freed, n)

        def store(pool, n):
            pool.wait_ge(res_ready, n + 1)
            pool.indirect_dma_start(out=out, out_offset=bass.IndirectOffsetOnAxis(
                ap=xs[:, n % 3, DIM:ROW].bitcast(I32), axis=0), in_=res[:, n % 2, :], in_offset=None,
                bounds_check=TOKENS - 1, oob_is_err=False).then_inc(stored[n % 2], 16)

        def slots():
            for slot in range(FIRST_SLOT, LAST_SLOT + 1):
                for g in range(GROUPS):
                    if 0 <= slot < TILES:
                        G_ = slot * GROUPS + g
                        yield slot, g, G_, range(group_start[G_], group_start[G_ + 1])
                    else:
                        yield slot, g, None, range(0)

        @block.sync
        def _(sp):
            for b in range(BATCH):
                sp.dma_start(xall[:, b * TPB:(b + 1) * TPB, 0:DIM], x_rows[:, b * TPB:(b + 1) * TPB, :])\
                    .then_inc(x_in[b], 16)
            sp.dma_start(wk[:], xwk_t.rearrange("(c p) n -> p c n", p=P)).then_inc(wk_in, 16)
            sp.dma_start(wv[:], xwv_t.rearrange("(c p) n -> p c n", p=P)).then_inc(wk_in, 16)
            sp.dma_start(ctxs[:], ctx_t.rearrange("(c p) n -> p c n", p=P)).then_inc(wk_in, 16)
            sp.dma_start(bcol[:], biases).then_inc(wk_in, 16)
            sp.dma_start(wq2[:], xwq.rearrange("(c p) n -> p c n", p=P)).then_inc(wk_in, 16)
            sp.dma_start(wo2[:], xwout_t.rearrange("(c p) n -> p c n", p=P)).then_inc(wk_in, 16)
            sp.dma_start(wout[:], wout_t.rearrange("(c p) n -> p c n", p=P)).then_inc(wo_in, 16)
            sp.wait_ge(logit_ready, TILES)
            sp.wait_ge(act_done, 1)
            sp.wait_ge(pe_done, 1)
            for e in range(EXP):
                sp.dma_start(wvs[:, e], w_v[e].rearrange("(c p) n -> p c n", p=P)).then_inc(ffn_w, 16)
                sp.dma_start(wps[:, e], w_proj[e].rearrange("(c p) n -> p c n", p=P)).then_inc(ffn_w, 16)
            sp.wait_ge(scattered, 16 * TILES)
            for n in range(SORTED):
                if n >= 3:
                    sp.wait_ge(res_ready, n - 2)
                    sp.wait_ge(stored[(n - 3) % 2], 16 * ((n - 3) // 2 + 1))
                sp.dma_start(xs[:, n % 3, :], sorted_rows[n * P:(n + 1) * P, :]).then_inc(xs_in[n % 3], 16)

        @block.gpsimd
        def _(pool):
            nc.gpsimd.memset(ident[:], 0.0).then_inc(consts, 1)
            nc.gpsimd.memset(tri[:], 1.0).then_inc(consts, 1)
            nc.gpsimd.memset(own[:], 1.0).then_inc(consts, 1)
            nc.gpsimd.memset(rowm[:], 0.0).then_inc(consts, 1)
            nc.gpsimd.memset(half[:], -0.5).then_inc(consts, 1)
            nc.gpsimd.memset(ones[:], 1.0).then_inc(consts, 1)
            nc.gpsimd.memset(pad_row[:], 0.0).then_inc(consts, 1)
            nc.gpsimd.memset(g2b[0:1, 0:1], 0.0).then_inc(consts, 1)
            pool.wait_ge(consts, 8)
            nc.gpsimd.affine_select(out=ident[:], in_=ident[:], compare_op=ALU.not_equal, fill=1.0, base=0,
                                    pattern=[[-1, P]], channel_multiplier=1).then_inc(consts, 1)
            nc.gpsimd.affine_select(out=tri[:], in_=tri[:], compare_op=ALU.is_gt, fill=0.0, base=0,
                                    pattern=[[1, P]], channel_multiplier=-1).then_inc(consts, 1)
            nc.gpsimd.affine_select(out=own[:], in_=own[:], compare_op=ALU.is_ge, fill=0.0, base=0,
                                    pattern=[[-XD, 8], [0, CPAD]], channel_multiplier=1).then_inc(own_ok, 1)
            for n in range(2):
                nc.gpsimd.affine_select(out=rowm[:, n:n + 1], in_=rowm[:, n:n + 1], compare_op=ALU.not_equal,
                                        fill=1.0, base=-n, pattern=[[0, 1]], channel_multiplier=1).then_inc(consts, 1)
            pool.wait_ge(own_ok, 1)
            nc.gpsimd.affine_select(out=own[:], in_=own[:], compare_op=ALU.is_ge, fill=0.0, base=XD - 1,
                                    pattern=[[XD, 8], [0, CPAD]], channel_multiplier=-1).then_inc(own_ok, 1)
            nc.gpsimd.iota(xall[:, :, DIM:ROW].bitcast(I32), pattern=[[P, TILES], [0, 1]], base=0,
                           channel_multiplier=1).then_inc(consts, 1)
            nc.gpsimd.iota(pad_row[:, DIM:ROW].bitcast(I32), pattern=[[0, 1]], base=TOKENS,
                           channel_multiplier=0).then_inc(consts, 1)
            pool.dma_start(g2b[0:1, :], g2.rearrange("(a n) -> a n", a=1)).then_inc(rows_in, 16)
            pool.dma_start(boutb[0:1, :], xbout.rearrange("(a n) -> a n", a=1)).then_inc(rows_in, 16)
            pool.dma_start(wrb[0:1, :, :], wr_t.rearrange("(a e) n -> a e n", a=1)).then_inc(rows_in, 16)
            pool.wait_ge(consts, 14)
            for n in range(SORTED):
                pool.dma_start(sorted_rows[n * P:(n + 1) * P, :], pad_row[:]).then_inc(pad_out, 16)
            pool.wait_ge(rows_in, 48)
            nc.gpsimd.partition_broadcast(g2b[:], g2b[0:1, :]).then_inc(spread, 1)
            nc.gpsimd.partition_broadcast(boutb[:], boutb[0:1, :]).then_inc(spread, 1)
            nc.gpsimd.partition_broadcast(wrb[:].rearrange("p e n -> p (e n)"),
                                          wrb[0:1].rearrange("p e n -> p (e n)")).then_inc(spread, 1)
            pool.wait_ge(stats_in, 1)
            nc.gpsimd.tensor_tensor(rstd[:], rin[:], half[:, 0:TILES], ALU.pow).then_inc(rstd_ok, 1)

            n_root = 0

            def root(which):
                nonlocal n_root
                n_root += 1
                pool.wait_ge(ln_step, n_root)
                nc.gpsimd.tensor_tensor(rs2[:], ri2[:], half[:, 0:1], ALU.pow).then_inc(ln_root, 1)

            diag = 0
            for slot, g, G_, ks in slots():
                for k in ks:
                    t, _, j = steps[k]
                    if j == t % TPB:
                        pool.wait_ge(p_ready, k + 1)
                        blk = pr[:, k % RING, :].rearrange("p (h q) -> p h q", h=HPG)
                        nc.gpsimd.affine_select(out=blk, in_=blk, compare_op=ALU.is_ge, fill=0.0, base=0,
                                                pattern=[[0, HPG], [1, P]], channel_multiplier=-1)\
                            .then_inc(masked, 1)
                for name, t, extra, job in side[slot, g]:
                    if name == "qkv":
                        pool.wait_ge(ssc_ready, t + 1)
                        if t >= 1:
                            pool.wait_ge(dve_freed, freed[qkv_job[t - 1] + NQ - 1][1])
                        nc.gpsimd.tensor_tensor(rn[:, 0:HEADS + 1], ssc[:, 0:HEADS + 1], half[:, 0:HEADS + 1],
                                                ALU.pow).then_inc(rn_ready, 1)
                        pool.wait_ge(qhi_ready, t + 1)
                        pool.wait_ge(qlo_ready, t + 1)
                        if t >= KV:
                            pool.wait_ge(pv_done, group_start[GROUPS * TPB * ((t - KV) // TPB + 1)])
                        vs = t % KV
                        nc.gpsimd.tensor_copy(vhi[:, vs, 0:DH], qhl[:, HEADS + 1, 0, :].bitcast(F32)).then_inc(v_ready, 1)
                        nc.gpsimd.tensor_copy(vlo[:, vs, 0:DH], qhl[:, HEADS + 1, 1, :].bitcast(F32)).then_inc(v_ready, 1)
                    elif name == "out_proj":
                        root("attn out")
                        pool.wait_ge(xa_ready, t + 1)
                        nc.gpsimd.tensor_tensor(xa[:], xa[:], g2b[:], ALU.mult).then_inc(xa_step, 1)
                        pool.wait_ge(xa_step, t + 1)
                        nc.gpsimd.tensor_tensor(xall[:, t, 0:DIM], xall[:, t, 0:DIM], xa[:], ALU.add)\
                            .then_inc(x1_ready, 1)
                        root("x1")
                        pool.wait_ge(z2_ready, t + 1)
                        nc.gpsimd.tensor_tensor(xall[:, t, 0:DIM], xall[:, t, 0:DIM], boutb[:], ALU.add)\
                            .then_inc(x1b_ready, 1)
                    elif name == "scores":
                        pool.wait_ge(rsm_ready, t + 1)
                        nc.gpsimd.tensor_tensor(sc[:], sc[:], rsm[:].unsqueeze(2).broadcast_to([P, XH, CPAD]),
                                                ALU.mult).then_inc(pn_ready, 1)
                    elif name == "xattn_out":
                        root("x2")

            pool.wait_ge(pad_out, 16 * SORTED)
            pool.wait_ge(x2_ready, TILES)
            pool.wait_ge(logit_ready, TILES)
            nc.gpsimd.iota(tnum_i[:], pattern=[[1, SORTED + 1]], base=0, channel_multiplier=0).then_inc(tile_num, 1)
            pool.wait_ge(pos_ready, 1)
            for t in range(TILES):
                pool.indirect_dma_start(out=sorted_rows, out_offset=bass.IndirectOffsetOnAxis(ap=pos_i[:, t:t + 1], axis=0),
                                        in_=xall[:, t, :], in_offset=None).then_inc(scattered, 16)
            for n in range(SORTED):
                pool.wait_ge(f_step, n + 1)
                nc.gpsimd.tensor_tensor(frs[:], fri[:], half[:, 0:1], ALU.pow).then_inc(f_root, 1)
                if n >= 1:
                    store(pool, n - 1)
            store(pool, SORTED - 1)
            for n in range(2):
                pool.wait_ge(stored[n], 16 * ((SORTED - n + 1) // 2))

        @block.scalar
        def _(act):
            act.dma_start(wqkv[:], wqkv_t.rearrange("(c p) n -> p c n", p=P)).then_inc(w_in, 16)
            act.dma_start(g1c[:], g1).then_inc(w_in, 16)
            for job, s in enumerate(setup):
                if s[0] == "kv":
                    continue
                act.wait_ge(side_ready, job + 1)
                w = W[job % WB]
                if s[0] == "g":
                    _, b, c, n = s
                    nc.scalar.copy(G[b][:, c, n * SB:(n + 1) * SB], w[:, 0:SB]).then_inc(act_freed, 1)
                elif s[0] == "bias":
                    _, b, n = s
                    if b > 0 and n == 0:
                        act.wait_ge(bias_step, 5 * b)
                    nc.scalar.copy(braw[:, n * SB:(n + 1) * SB], w[:, 0:SB]).then_inc(act_freed, 1)
                else:
                    _, b, n = s
                    nc.scalar.copy(VP[b][:, n, :], w[:, 0:DIM]).then_inc(act_freed, 1)

            for slot, g, G_, ks in slots():
                for k in ks:
                    act.wait_ge(s_ready, k + 1)
                    if k >= RING:
                        act.wait_ge(pl_ready, k - RING + 1)
                    nc.scalar.activation(pr[:, k % RING, :], S[k % 2][:], ACT.Exp, scale=SIM_SCALE)\
                        .then_inc(p_ready, 1)
                if G_ is not None:
                    act.wait_ge(pv_done, group_start[G_ + 1])
                    if G_ >= 2:
                        act.wait_ge(rl_ready, G_ - 1)
                    nc.scalar.copy(oT[0:DH + 1, G_ % 2, :], O[G_ % 2][0:DH + 1, :]).then_inc(ot_ready, 1)
                for name, t, extra, job in side[slot, g]:
                    if name == "z_turn":
                        act.wait_ge(side_ready, job + 1)
                        if t >= 1:
                            act.wait_ge(side_ready, qkv_job[t - 1] + NQ)
                        nc.scalar.copy(zT[:].rearrange("p c n -> p (c n)"), W[job % WB][:, 0:DIM]).then_inc(act_freed, 1)
                    elif name == "qkv":
                        for n in range(NQ):
                            act.wait_ge(side_ready, job + n + 1)
                            if t >= 1 and n == 0:
                                act.wait_ge(ss_ready, NQ * t)
                            nc.scalar.activation(sq[:, n, :], W[(job + n) % WB][:, 0:QB], ACT.Square).then_inc(sq_ready, 1)
                        act.wait_ge(dve_freed, freed[job + NQ - 1][1])
                        if t >= 1:
                            act.wait_ge(side_ready, turn_job[t - 1] + 5)
                            act.wait_ge(v_ready, 2 * t)
                            act.wait_ge(kdup_ready, 2 * t)
                        nc.scalar.copy(qhl[:, :, 0, :], qn[:]).then_inc(qhi_ready, 1)
                    elif name == "q_turn":
                        for n in (0, 2):
                            act.wait_ge(side_ready, job + n + 1)
                            if t >= 2:
                                act.wait_ge(s_ready, group_start[GROUPS * (t - 1)])
                            nc.scalar.copy(qT[t % 2][:, 4 * n:4 * n + 4, :].rearrange("p h q -> p (h q)"),
                                           W[(job + n) % WB][:]).then_inc(act_freed, 1)
                        act.wait_ge(side_ready, job + 5)
                        if t >= KV:
                            act.wait_ge(s_ready, group_start[GROUPS * TPB * ((t - KV) // TPB + 1)])
                        nc.scalar.copy(kT[:, t % KV].rearrange("p a k -> p (a k)"),
                                       W[(job + 4) % WB][:, 0:2 * P]).then_inc(act_freed, 1)
                    elif name == "out_turn":
                        for n in range(2):
                            act.wait_ge(side_ready, job + n + 1)
                            if t >= 1 and n == 0:
                                act.wait_ge(side_ready, proj_job[t - 1] + 1)
                            nc.scalar.copy(onT[:, 4 * n:4 * n + 4, :].rearrange("p c q -> p (c q)"),
                                           W[(job + n) % WB][:]).then_inc(act_freed, 1)
                    elif name == "z2_turn":
                        act.wait_ge(side_ready, job + 1)
                        if t >= 1:
                            act.wait_ge(side_ready, score_job[t - 1] + 4)
                        nc.scalar.copy(z2T[:].rearrange("p c n -> p (c n)"), W[job % WB][:, 0:DIM]).then_inc(act_freed, 1)
                    elif name == "scores":
                        act.wait_ge(sc_ready, 4 * (t + 1))
                        nc.scalar.activation(sc[:], sc[:], ACT.Exp).then_inc(pe_ready, 1)
                    elif name == "probs_turn":
                        for n in range(3):
                            act.wait_ge(side_ready, job + n + 1)
                            if t >= 1 and n == 0:
                                act.wait_ge(side_ready, xout_job[t - 1] + 1)
                            c = min(4, HKC - 4 * n)
                            nc.scalar.copy(pT[:, 4 * n:4 * n + c, :].rearrange("p c q -> p (c q)"),
                                           W[(job + n) % WB][:, 0:c * P]).then_inc(act_freed, 1)
            act.wait_ge(act_freed, max(n for e, n in freed if e == "act"))
            act.wait_ge(pe_ready, TILES)
            act.wait_ge(qhi_ready, TILES)
            act.sem_inc(act_done, 1)

            for n in range(SORTED + 1):
                if n < SORTED:
                    act.wait_ge(f_turn, n + 1)
                    if n >= 1:
                        act.wait_ge(up_ready, 2 * n)
                    nc.scalar.copy(fzT[:].rearrange("p c n -> p (c n)"), W[0][:, 0:DIM]).then_inc(fzT_ready, 1)
                if n >= 1:
                    for c in range(2):
                        act.wait_ge(h_turned, 2 * (n - 1) + c + 1)
                        if n >= 2 and c == 0:
                            act.wait_ge(down_ready, n - 1)
                        nc.scalar.copy(hT[:, 4 * c:4 * c + 4, :].rearrange("p c q -> p (c q)"), W[2 + c][:])\
                            .then_inc(hT_ready, 1)
                if n < SORTED:
                    for c in range(2):
                        act.wait_ge(up_ready, 2 * n + 1)
                        if n >= 2:
                            act.wait_ge(h_ready, 2 * (n - 1))
                        nc.scalar.activation(gate[:, n % 2, c * 512:(c + 1) * 512], S[c][:], ACT.Silu)\
                            .then_inc(gate_ready, 1)

        @block.vector
        def _(dve):
            n_ln = 0
            n_self = 0

            def own_step(ins):
                nonlocal n_self
                n_self += 1
                ins.then_inc(ln_self, 1)
                dve.wait_ge(ln_self, n_self)

            def norm_root(src):
                nonlocal n_ln
                own_step(nc.vector.bn_stats(st2[:], src))
                own_step(nc.vector.bn_aggr(mv2[:], st2[:]))
                n_ln += 1
                nc.vector.tensor_scalar(ri2[:], mv2[:, 1:2], EPS, None, ALU.add).then_inc(ln_step, 1)
                dve.wait_ge(ln_root, n_ln)

            nc.vector.memset(floor[:, 0:HEADS], 3.90625e-27).then_inc(dconst, 1)
            nc.vector.memset(floor[:, HEADS:HEADS + 2], 1e-24).then_inc(dconst, 1)
            nc.vector.memset(rn[:], 1.0).then_inc(dconst, 1)
            nc.vector.memset(kvT[:], 0.0).then_inc(dconst, 1)
            nc.vector.memset(braw[:], 0.0).then_inc(dconst, 1)
            dve.wait_ge(dconst, 5)

            for t in range(TILES):
                dve.wait_ge(x_in[t // TPB], 16)
                nc.vector.bn_stats(stat[:, t, :], xall[:, t, 0:DIM]).then_inc(stats_ok, 1)
            for t in range(TILES):
                dve.wait_ge(stats_ok, t + 1)
                nc.vector.bn_aggr(mv[:, t, :], stat[:, t, :]).then_inc(stats_ok, 1)
            dve.wait_ge(stats_ok, 2 * TILES)
            nc.vector.tensor_scalar(rin[:], mv[:, :, 1], 1.0 + EPS, EPS * EPS, ALU.mult, ALU.add).then_inc(stats_in, 1)
            dve.wait_ge(w_in, 32)
            for c in range(CH):
                nc.vector.tensor_scalar(wqkv[:, c, :], wqkv[:, c, :], g1c[:, c:c + 1], None, ALU.mult).then_inc(wq_scaled, 1)

            dve.wait_ge(wk_in, 16 * 6)
            for m in range(CH):
                nc.vector.tensor_copy(bqb[:, m, :], bcol[:, 0, m:m + 1].broadcast_to([P, P])).then_inc(bd_ready, 1)
            for m in range(4):
                dve.wait_ge(side_ready, m + 1)
                src = W[m % WB][:, 0:BATCH * CTX].rearrange("p (b k) -> p b k", b=BATCH)
                nc.vector.tensor_scalar(kvT[:, m, :, 0:CTX], src, bcol[:, 1 + m // CH, m % CH:m % CH + 1],
                                        0.25 if m < CH else 1.0, ALU.add, ALU.mult).then_inc(dve_freed, 1)
            dve.wait_ge(dve_freed, 4)
            dve.wait_ge(own_ok, 2)
            dve.wait_ge(consts, 14)
            for b in range(BATCH):
                if b > 0:
                    dve.wait_ge(side_ready, 4 + 22 * b)
                for m in range(CH):
                    for dst, src in ((kbd, m), (vbd, CH + m)):
                        nc.vector.tensor_tensor(dst[:, m], own[:], kvT[:, src, b, :].unsqueeze(1).broadcast_to([P, 8, CPAD]),
                                                ALU.mult).then_inc(bd_ready, 1)
                dve.wait_ge(act_freed, 22 * b + 12)
                pads = braw[:].rearrange("p (h k) -> p h k", k=CPAD)[:, :, CTX:CPAD]
                nc.vector.memset(pads, NEG).then_inc(bias_step, 1)
                dve.wait_ge(bias_step, 5 * b + 1)
                nc.vector.tensor_copy(bhi[:], braw[:]).then_inc(bias_step, 1)
                dve.wait_ge(bias_step, 5 * b + 2)
                nc.vector.tensor_tensor(blo[:], braw[:], bhi[:].bitcast(F32), ALU.subtract).then_inc(bias_step, 1)
                dve.wait_ge(bias_step, 5 * b + 3)
                nc.vector.tensor_scalar(blo[:], blo[:], rowm[:, 1:2], None, ALU.mult).then_inc(bias_step, 1)
                dve.wait_ge(bias_step, 5 * b + 4)
                nc.vector.scalar_tensor_tensor(out=BI[b][:], in0=bhi[:].bitcast(F32), scalar=rowm[:, 0:1], in1=blo[:],
                                               op0=ALU.mult, op1=ALU.add).then_inc(bias_step, 1)
            nc.vector.tensor_scalar(pick[:], ones[:], rowm[:, 0:1], rowm[:, 1:2], ALU.mult, ALU.add).then_inc(bias_step, 1)
            dve.wait_ge(bias_step, 5 * BATCH + 1)

            dve.wait_ge(side_ready, len(setup))
            dve.wait_ge(act_freed, len(setup) - 4)
            nc.vector.memset(vhi[:, :, DH:DH + 2].bitcast(F32), 1.0).then_inc(dconst, 1)
            nc.vector.memset(vlo[:, :, DH:DH + 2].bitcast(F32), 0.0).then_inc(dconst, 1)
            dve.wait_ge(rstd_ok, 1)

            diag = 0
            for slot, g, G_, ks in slots():
                for k in ks:
                    t, _, j = steps[k]
                    if j == t % TPB:
                        diag += 1
                        dve.wait_ge(masked, diag)
                    else:
                        dve.wait_ge(p_ready, k + 1)
                    if k >= RING:
                        dve.wait_ge(pv_done, k - RING + 1)
                    nc.vector.tensor_copy(ph[:, k % RING, :], pr[:, k % RING, :]).then_inc(ph_ready, 1)
                    dve.wait_ge(ph_ready, k + 1)
                    nc.vector.tensor_tensor(pl[:, k % RING, :], pr[:, k % RING, :], ph[:, k % RING, :].bitcast(F32),
                                            ALU.subtract).then_inc(pl_ready, 1)
                for name, t, extra, job in side[slot, g]:
                    if name == "norm_x":
                        if t >= 2:
                            dve.wait_ge(side_ready, zturn_job[t - 2] + 1)
                        nc.vector.tensor_scalar(z[t % 2][:], xall[:, t, 0:DIM], mv[:, t, 0:1], rstd[:, t:t + 1],
                                                ALU.subtract, ALU.mult).then_inc(z_ready, 1)
                    elif name == "qkv":
                        for n in range(NQ):
                            dve.wait_ge(sq_ready, NQ * t + n + 1)
                            nc.vector.tensor_reduce(ss[:, n * HPB:(n + 1) * HPB],
                                                    sq[:, n, :].rearrange("p (h d) -> p h d", d=DH), AX.X, ALU.add)\
                                .then_inc(ss_ready, 1)
                        dve.wait_ge(ss_ready, NQ * (t + 1))
                        if t >= 1:
                            dve.wait_ge(rn_ready, t)
                        nc.vector.tensor_tensor(ssc[:], ss[:], floor[:], ALU.max).then_inc(ssc_ready, 1)
                        dve.wait_ge(rn_ready, t + 1)
                        if t >= 1:
                            dve.wait_ge(qhi_ready, t)
                            dve.wait_ge(qlo_ready, t)
                        for n in range(NQ):
                            src = W[(job + n) % WB][:, 0:QB].rearrange("p (h d) -> p h d", d=DH)
                            nc.vector.tensor_tensor(qn[:, n * HPB:(n + 1) * HPB, :], src,
                                                    rn[:, n * HPB:(n + 1) * HPB].unsqueeze(2).broadcast_to([P, HPB, DH]),
                                                    ALU.mult).then_inc(dve_freed, 1)
                        dve.wait_ge(qhi_ready, t + 1)
                        nc.vector.tensor_tensor(qhl[:, :, 1, :], qn[:], qhl[:, :, 0, :].bitcast(F32), ALU.subtract)\
                            .then_inc(qlo_ready, 1)
                        dve.wait_ge(qlo_ready, t + 1)
                        for n in range(2):
                            nc.vector.tensor_copy(kdup[:, n], qhl[:, HEADS, n, :].bitcast(F32).unsqueeze(1).broadcast_to([P, 2, DH]))\
                                .then_inc(kdup_ready, 1)
                    elif name == "q_turn":
                        for n in (1, 3):
                            dve.wait_ge(side_ready, job + n + 1)
                            if t >= 2:
                                dve.wait_ge(s_ready, group_start[GROUPS * (t - 1)])
                            nc.vector.tensor_copy(qT[t % 2][:, 4 * n:4 * n + 4, :].rearrange("p h q -> p (h q)"),
                                                  W[(job + n) % WB][:]).then_inc(dve_freed, 1)
                    elif name == "heads_out":
                        dve.wait_ge(side_ready, job + 1)
                        src = W[job % WB][:, 0:HPG * (DH + 1)].rearrange("p (h d) -> p h d", d=DH + 1)
                        nc.vector.reciprocal(rl[:], src[:, :, DH]).then_inc(rl_ready, 1)
                        dve.wait_ge(rl_ready, GROUPS * t + extra + 1)
                        if t >= 2 and extra == 0:
                            dve.wait_ge(side_ready, oturn_job[t - 2] + 2)
                        nc.vector.tensor_tensor(
                            on[t % 2][:, extra * DIM:(extra + 1) * DIM].rearrange("p (h d) -> p h d", d=DH),
                            src[:, :, 0:DH], rl[:].unsqueeze(2).broadcast_to([P, HPG, DH]), ALU.mult)\
                            .then_inc(dve_freed, 1)
                    elif name == "out_proj":
                        dve.wait_ge(side_ready, job + 1)
                        norm_root(W[job % WB][:, 0:DIM])
                        if t >= 1:
                            dve.wait_ge(x1_ready, t)
                        nc.vector.tensor_scalar(xa[:], W[job % WB][:, 0:DIM], mv2[:, 0:1], rs2[:], ALU.subtract, ALU.mult)\
                            .then_inc(dve_freed, 1)
                        dve.wait_ge(dve_freed, freed[job][1])
                        dve.sem_inc(xa_ready, 1)
                        dve.wait_ge(x1_ready, t + 1)
                        norm_root(xall[:, t, 0:DIM])
                        if t >= 1:
                            dve.wait_ge(side_ready, z2turn_job[t - 1] + 1)
                        nc.vector.tensor_scalar(z2[:], xall[:, t, 0:DIM], mv2[:, 0:1], rs2[:], ALU.subtract, ALU.mult)\
                            .then_inc(z2_ready, 1)
                    elif name == "scores":
                        if t >= 1:
                            dve.wait_ge(side_ready, pturn_job[t - 1] + 3)
                        for n in range(4):
                            dve.wait_ge(side_ready, job + n + 1)
                            src = W[(job + n) % WB][:, 0:SB].rearrange("p (h k) -> p h k", k=CPAD)
                            nc.vector.tensor_reduce(mx[:, 4 * n:4 * n + 4], src, AX.X, ALU.max).then_inc(mx_ready, 1)
                            dve.wait_ge(mx_ready, 4 * t + n + 1)
                            nc.vector.tensor_tensor(sc[:, 4 * n:4 * n + 4, :], src,
                                                    mx[:, 4 * n:4 * n + 4].unsqueeze(2).broadcast_to([P, 4, CPAD]),
                                                    ALU.subtract).then_inc(dve_freed, 1)
                        dve.wait_ge(dve_freed, freed[job + 3][1])
                        dve.sem_inc(sc_ready, 4)
                        dve.wait_ge(pe_ready, t + 1)
                        nc.vector.tensor_reduce(sm[:], sc[:], AX.X, ALU.add).then_inc(sm_ready, 1)
                        dve.wait_ge(sm_ready, t + 1)
                        if t >= 1:
                            dve.wait_ge(pn_ready, t)
                        nc.vector.reciprocal(rsm[:], sm[:]).then_inc(rsm_ready, 1)
                    elif name == "xattn_out":
                        dve.wait_ge(side_ready, job + 1)
                        dve.wait_ge(x1b_ready, t + 1)
                        nc.vector.tensor_tensor(xall[:, t, 0:DIM], xall[:, t, 0:DIM], W[job % WB][:, 0:DIM], ALU.add)\
                            .then_inc(dve_freed, 1)
                        dve.wait_ge(dve_freed, freed[job][1])
                        dve.sem_inc(x2_ready, 1)
                        norm_root(xall[:, t, 0:DIM])
                        nc.vector.tensor_scalar(z3[:], xall[:, t, 0:DIM], mv2[:, 0:1], rs2[:], ALU.subtract, ALU.mult)\
                            .then_inc(z3_ready, 1)
                        dve.wait_ge(z3_ready, t + 1)
                        for e in range(EXP):
                            last = nc.vector.tensor_tensor_reduce(junk[:], z3[:], wrb[:, e, :], 1.0, 0.0, ALU.mult, ALU.add,
                                                                  logits[:, t, e:e + 1])
                            own_step(last)
                        dve.sem_inc(logit_ready, 1)

            n_r = 0

            def r(ins):
                nonlocal n_r
                n_r += 1
                ins.then_inc(route, 1)
                dve.wait_ge(route, n_r)

            dve.wait_ge(act_done, 1)
            dve.wait_ge(pe_done, 1)
            r(nc.vector.tensor_reduce(best[:], logits[:], AX.X, ALU.max))
            r(nc.vector.tensor_tensor(eq[:], logits[:], best[:].unsqueeze(2).broadcast_to([P, TILES, EXP]), ALU.is_equal))
            r(nc.vector.memset(left[:], 1.0))
            for e in range(EXP - 1):
                r(nc.vector.tensor_tensor(oh[:, :, e], eq[:, :, e], left[:], ALU.mult))
                r(nc.vector.tensor_tensor(left[:], left[:], oh[:, :, e], ALU.subtract))
            r(nc.vector.tensor_copy(oh[:, :, EXP - 1], left[:]))
            N_OH = n_r
            assert N_OH == ONEHOT_STEPS
            dve.wait_ge(counted, 1)
            r(nc.vector.tensor_copy(tot[:], W[1][:, 0:TILES * EXP].rearrange("p (t e) -> p t e", e=EXP)))
            r(nc.vector.memset(base[:, 0, :], 0.0))
            for t in range(TILES):
                r(nc.vector.tensor_tensor(base[:, t + 1, :], base[:, t, :], tot[:, t, :], ALU.add))
            r(nc.vector.tensor_scalar(cnt_i[:], base[:, TILES, :], float(P - 1), None, ALU.add))
            r(nc.vector.tensor_scalar(cnt_s[:], cnt_i[:], 7, None, ALU.arith_shift_right))
            r(nc.vector.tensor_copy(cnt_f[:], cnt_s[:]))
            r(nc.vector.memset(end[:, 0:1], 0.0))
            for e in range(EXP):
                r(nc.vector.tensor_tensor(end[:, e + 1:e + 2], end[:, e:e + 1], cnt_f[:, e:e + 1], ALU.add))
            r(nc.vector.tensor_scalar(off[:], end[:, 0:EXP], float(P), None, ALU.mult))
            r(nc.vector.tensor_tensor(rank[:], base[:, 0:TILES, :], W[0][:, 0:TILES * EXP].rearrange("p (t e) -> p t e", e=EXP), ALU.add))
            r(nc.vector.tensor_tensor(rank[:], rank[:], off[:].unsqueeze(1).broadcast_to([P, TILES, EXP]), ALU.add))
            r(nc.vector.tensor_tensor(rank[:], rank[:], oh[:], ALU.mult))
            r(nc.vector.tensor_reduce(posf[:], rank[:], AX.X, ALU.add))
            nc.vector.tensor_copy(pos_i[:], posf[:]).then_inc(pos_ready, 1)
            dve.wait_ge(tile_num, 1)
            r(nc.vector.tensor_copy(tnum[:], tnum_i[:]))
            r(nc.vector.tensor_scalar(ecmp[:], tnum[:], end[:, 1:2], None, ALU.is_ge))
            for e in range(1, EXP - 1):
                r(nc.vector.scalar_tensor_tensor(out=ecmp[:], in0=tnum[:], scalar=end[:, e + 1:e + 2], in1=ecmp[:],
                                                 op0=ALU.is_ge, op1=ALU.add))
            r(nc.vector.tensor_copy(expert_i[:], ecmp[:]))
            assert n_r == ROUTE_STEPS

            n_f = 0

            def f(ins):
                nonlocal n_f
                n_f += 1
                ins.then_inc(f_self, 1)
                dve.wait_ge(f_self, n_f)

            for n in range(SORTED + 1):
                if n < SORTED:
                    src = xs[:, n % 3, 0:DIM]
                    dve.wait_ge(xs_in[n % 3], 16 * (n // 3 + 1))
                    f(nc.vector.bn_stats(fst[:], src))
                    f(nc.vector.bn_aggr(fmv[:], fst[:]))
                    nc.vector.tensor_scalar(fri[:], fmv[:, 1:2], EPS, None, ALU.add).then_inc(f_step, 1)
                    dve.wait_ge(f_root, n + 1)
                    if n >= 1:
                        dve.wait_ge(f_turn, n)
                    nc.vector.tensor_scalar(fz[:], src, fmv[:, 0:1], frs[:], ALU.subtract, ALU.mult).then_inc(fz_ready, 1)
                if n >= 1:
                    dve.wait_ge(down_ready, n)
                    if n >= 3:
                        dve.wait_ge(stored[(n - 1) % 2], 16 * ((n - 1) // 2))
                    nc.vector.tensor_tensor(res[:, (n - 1) % 2, :], xs[:, (n - 1) % 3, 0:DIM], W[1][:, 0:DIM], ALU.add)\
                        .then_inc(res_ready, 1)
                if n < SORTED:
                    for c in range(2):
                        dve.wait_ge(gate_ready, 2 * n + c + 1)
                        dve.wait_ge(up_ready, 2 * n + 2)
                        if n >= 2:
                            dve.wait_ge(h_turned, 2 * (n - 1))
                        nc.vector.tensor_tensor(hh[:, n % 2, c * 512:(c + 1) * 512], gate[:, n % 2, c * 512:(c + 1) * 512],
                                                O[c][:], ALU.mult).then_inc(h_ready, 1)

        @block.tensor
        def _(pe):
            pe.wait_ge(wk_in, 16 * 6)
            pe.wait_ge(consts, 14)
            for job, s in enumerate(setup):
                freed_wait(pe, job)
                w = W[job % WB]
                if s[0] == "kv":
                    m = s[1]
                    wt = wk if m < CH else wv
                    for c in range(CH):
                        mm = nc.tensor.matmul(w[:, 0:BATCH * CTX], wt[:, c, (m % CH) * P:(m % CH + 1) * P], ctxs[:, c, :],
                                              start=c == 0, stop=c == CH - 1)
                elif s[0] == "g":
                    _, b, c, n = s
                    pe.wait_ge(bd_ready, 2 + 4 * (b + 1))
                    mm = nc.tensor.matmul(w[:, 0:SB], wq2[:, n // 2, c * P:(c + 1) * P],
                                          kbd[:, n // 2, 4 * (n % 2):4 * (n % 2) + 4, :].rearrange("p h k -> p (h k)"),
                                          start=True, stop=True)
                elif s[0] == "bias":
                    _, b, n = s
                    mm = nc.tensor.matmul(w[:, 0:SB], bqb[:, n // 2, :],
                                          kbd[:, n // 2, 4 * (n % 2):4 * (n % 2) + 4, :].rearrange("p h k -> p (h k)"),
                                          start=True, stop=True)
                else:
                    _, b, n = s
                    m, cc = n // 5, n % 5
                    mm = nc.tensor.matmul(w[:, 0:DIM], vbd[:, m].rearrange("p h k -> p (h k)")[:, cc * P:(cc + 1) * P],
                                          wo2[:, m, :], start=True, stop=True)
                mm.then_inc(side_ready, 1)
            pe.wait_ge(wq_scaled, CH)
            pe.wait_ge(wo_in, 16)
            pe.wait_ge(dconst, 7)
            pe.wait_ge(bias_step, 5 * BATCH + 1)

            def scores_of(k):
                t, g, j = steps[k]
                if k >= 2:
                    pe.wait_ge(p_ready, k - 1)
                if g == 0 and j == 0:
                    pe.wait_ge(act_freed, freed[turn_job[t] + 4][1])
                    pe.wait_ge(dve_freed, freed[turn_job[t] + 3][1])
                ks = (t - t % TPB + j) % KV
                q = qT[t % 2][:, HPG * g:HPG * (g + 1), :].rearrange("p h q -> p (h q)")
                nc.tensor.matmul(S[k % 2][:], kT[:, ks, 0, :], q, start=True, stop=False)
                nc.tensor.matmul(S[k % 2][:], kT[:, ks, 1, :], q, start=False, stop=True).then_inc(s_ready, 1)

            def values_of(k):
                t, g, j = steps[k]
                G_ = GROUPS * t + g
                o = O[G_ % 2][0:DH + 1, :]
                if j == 0:
                    if G_ >= 2:
                        pe.wait_ge(ot_ready, G_ - 1)
                    if g == 0:
                        pe.wait_ge(v_ready, 2 * (t + 1))
                vs = (t - t % TPB + j) % KV
                last = j == t % TPB
                pe.wait_ge(ph_ready, k + 1)
                nc.tensor.matmul(o, vhi[:, vs, 0:DH + 1], ph[:, k % RING, :], start=j == 0, stop=False)
                nc.tensor.matmul(o, vlo[:, vs, 0:DH + 1], ph[:, k % RING, :], start=False, stop=False)
                pe.wait_ge(pl_ready, k + 1)
                nc.tensor.matmul(o, vhi[:, vs, 0:DH + 1], pl[:, k % RING, :], start=False, stop=last).then_inc(pv_done, 1)

            for slot, g, G_, ks in slots():
                if slot == 0 and g == 0:
                    scores_of(0)
                    scores_of(1)
                for k in ks:
                    values_of(k)
                    if k + 2 < N_STEPS:
                        scores_of(k + 2)
                for name, t, extra, job in side[slot, g]:
                    b = t // TPB
                    if name == "z_turn":
                        pe.wait_ge(z_ready, t + 1)
                        freed_wait(pe, job)
                        for c in range(CH):
                            mm = nc.tensor.transpose(W[job % WB][:, c * P:(c + 1) * P], z[t % 2][:, c * P:(c + 1) * P], ident[:])
                        mm.then_inc(side_ready, 1)
                    elif name == "qkv":
                        pe.wait_ge(act_freed, freed[zturn_job[t]][1])
                        for n in range(NQ):
                            freed_wait(pe, job + n)
                            for c in range(CH):
                                mm = nc.tensor.matmul(W[(job + n) % WB][:, 0:QB], zT[:, c, :], wqkv[:, c, n * QB:(n + 1) * QB],
                                                      start=c == 0, stop=c == CH - 1)
                            mm.then_inc(side_ready, 1)
                    elif name == "q_turn":
                        pe.wait_ge(qlo_ready, t + 1)
                        for n in range(4):
                            freed_wait(pe, job + n)
                            for h in range(4):
                                mm = nc.tensor.transpose(W[(job + n) % WB][:, h * P:(h + 1) * P],
                                                         qhl[:, 4 * n + h].rearrange("p a d -> p (a d)").bitcast(F32), ident[:])
                            mm.then_inc(side_ready, 1)
                        pe.wait_ge(kdup_ready, 2 * (t + 1))
                        freed_wait(pe, job + 4)
                        for h in range(2):
                            mm = nc.tensor.transpose(W[(job + 4) % WB][:, h * P:(h + 1) * P],
                                                     kdup[:, h].rearrange("p a d -> p (a d)"), ident[:])
                        mm.then_inc(side_ready, 1)
                    elif name == "heads_out":
                        pe.wait_ge(ot_ready, GROUPS * t + extra + 1)
                        freed_wait(pe, job)
                        for h in range(HPG):
                            mm = nc.tensor.transpose(W[job % WB][:, h * (DH + 1):(h + 1) * (DH + 1)],
                                                     oT[0:DH + 1, (GROUPS * t + extra) % 2, h * P:(h + 1) * P],
                                                     ident[0:DH + 1, 0:DH + 1])
                        mm.then_inc(side_ready, 1)
                    elif name == "out_turn":
                        pe.wait_ge(dve_freed, freed[heads3_job[t]][1])
                        for n in range(2):
                            freed_wait(pe, job + n)
                            for c in range(4):
                                mm = nc.tensor.transpose(W[(job + n) % WB][:, c * P:(c + 1) * P],
                                                         on[t % 2][:, (4 * n + c) * P:(4 * n + c + 1) * P], ident[:])
                            mm.then_inc(side_ready, 1)
                    elif name == "out_proj":
                        pe.wait_ge(act_freed, freed[oturn_job[t] + 1][1])
                        freed_wait(pe, job)
                        for c in range(8):
                            mm = nc.tensor.matmul(W[job % WB][:, 0:DIM], onT[:, c, :], wout[:, c, :], start=c == 0, stop=c == 7)
                        mm.then_inc(side_ready, 1)
                    elif name == "z2_turn":
                        pe.wait_ge(z2_ready, t + 1)
                        freed_wait(pe, job)
                        for c in range(CH):
                            mm = nc.tensor.transpose(W[job % WB][:, c * P:(c + 1) * P], z2[:, c * P:(c + 1) * P], ident[:])
                        mm.then_inc(side_ready, 1)
                    elif name == "scores":
                        pe.wait_ge(act_freed, freed[z2turn_job[t]][1])
                        for n in range(4):
                            freed_wait(pe, job + n)
                            w = W[(job + n) % WB][:, 0:SB]
                            nc.tensor.matmul(w, pick[:], BI[b][:, n * SB:(n + 1) * SB], start=True, stop=False)
                            for c in range(CH):
                                mm = nc.tensor.matmul(w, z2T[:, c, :], G[b][:, c, n * SB:(n + 1) * SB],
                                                      start=False, stop=c == CH - 1)
                            mm.then_inc(side_ready, 1)
                    elif name == "probs_turn":
                        pe.wait_ge(pn_ready, t + 1)
                        pn = sc[:].rearrange("p h k -> p (h k)")
                        for n in range(3):
                            freed_wait(pe, job + n)
                            for c in range(4 * n, min(4 * n + 4, HKC)):
                                mm = nc.tensor.transpose(W[(job + n) % WB][:, (c - 4 * n) * P:(c - 4 * n + 1) * P],
                                                         pn[:, c * P:(c + 1) * P], ident[:])
                            mm.then_inc(side_ready, 1)
                    elif name == "xattn_out":
                        pe.wait_ge(act_freed, freed[pturn_job[t] + 2][1])
                        freed_wait(pe, job)
                        for c in range(HKC):
                            mm = nc.tensor.matmul(W[job % WB][:, 0:DIM], pT[:, c, :], VP[b][:, c, :], start=c == 0, stop=c == HKC - 1)
                        mm.then_inc(side_ready, 1)
            pe.wait_ge(side_ready, N_SIDE)
            pe.sem_inc(pe_done, 1)

            pe.wait_ge(route, ONEHOT_STEPS)
            oh2 = oh[:].rearrange("p t e -> p (t e)")
            nc.tensor.matmul(W[0][:, 0:TILES * EXP], tri[:], oh2, start=True, stop=True)
            nc.tensor.matmul(W[1][:, 0:TILES * EXP], ones[:], oh2, start=True, stop=True).then_inc(counted, 1)
            pe.wait_ge(route, ROUTE_STEPS)
            pe.wait_ge(ffn_w, 16 * 2 * EXP)

            def turn_rows(n):
                pe.wait_ge(fz_ready, n + 1)
                if n >= 1:
                    pe.wait_ge(fzT_ready, n)
                for c in range(CH):
                    mm = nc.tensor.transpose(W[0][:, c * P:(c + 1) * P], fz[:, c * P:(c + 1) * P], ident[:])
                mm.then_inc(f_turn, 1)

            def up(n):
                expert = pe.value_load(expert_i[0:1, n:n + 1], min_val=0, max_val=EXP - 1)
                pe.wait_ge(fzT_ready, n + 1)
                flat = wvs[:].rearrange("p e c n -> p (e c n)")
                for half_, banks in ((0, S), (1, O)):
                    for q in range(2):
                        if n >= 1:
                            pe.wait_ge(gate_ready if half_ == 0 else h_ready, 2 * (n - 1) + q + 1)
                        for c in range(CH):
                            at = expert * (CH * 2 * HID) + (c * 2 * HID + half_ * HID + q * 512)
                            mm = nc.tensor.matmul(banks[q][:], fzT[:, c, :], flat[:, bass.ds(at, 512)],
                                                  start=c == 0, stop=c == CH - 1)
                    mm.then_inc(up_ready, 1)
                return expert

            def down(n, expert):
                for q in range(2):
                    pe.wait_ge(h_ready, 2 * n + 2)
                    if n >= 1:
                        pe.wait_ge(hT_ready, 2 * (n - 1) + q + 1)
                    for c in range(4):
                        mm = nc.tensor.transpose(W[2 + q][:, c * P:(c + 1) * P],
                                                 hh[:, n % 2, (4 * q + c) * P:(4 * q + c + 1) * P], ident[:])
                    mm.then_inc(h_turned, 1)
                if n >= 1:
                    pe.wait_ge(res_ready, n)
                flat = wps[:].rearrange("p e c n -> p (e c n)")
                for c in range(HID // P):
                    pe.wait_ge(hT_ready, 2 * n + c // 4 + 1)
                    at = expert * (HID // P * DIM) + c * DIM
                    mm = nc.tensor.matmul(W[1][:, 0:DIM], hT[:, c, :], flat[:, bass.ds(at, DIM)],
                                          start=c == 0, stop=c == HID // P - 1)
                mm.then_inc(down_ready, 1)

            before = None
            for n in range(SORTED + 1):
                if n < SORTED:
                    turn_rows(n)
                if n >= 1:
                    down(n - 1, before)
                if n < SORTED:
                    before = up(n)



ONEHOT_STEPS = 10
ROUTE_STEPS = 46


def _job_tables():
    freed = [("act", 0)] * 48
    gaps = plan_side(48, freed)
    at = {}
    for here in gaps.values():
        for name, t, extra, job in here:
            at[name, t, extra] = job
    return at


_AT = _job_tables()
zturn_job = {t: _AT["z_turn", t, 0] for t in range(TILES)}
qkv_job = {t: _AT["qkv", t, 0] for t in range(TILES)}
turn_job = {t: _AT["q_turn", t, 0] for t in range(TILES)}
heads3_job = {t: _AT["heads_out", t, 3] for t in range(TILES)}
oturn_job = {t: _AT["out_turn", t, 0] for t in range(TILES)}
proj_job = {t: _AT["out_proj", t, 0] for t in range(TILES)}
z2turn_job = {t: _AT["z2_turn", t, 0] for t in range(TILES)}
score_job = {t: _AT["scores", t, 0] for t in range(TILES)}
pturn_job = {t: _AT["probs_turn", t, 0] for t in range(TILES)}
xout_job = {t: _AT["xattn_out", t, 0] for t in range(TILES)}


def kernel(**inputs):
    import numpy as np
    import concourse.bacc as bacc
    from concourse.bass_utils import run_bass_kernel_spmd

    i = {k: np.asarray(v) for k, v in inputs.items()}
    wqkv = np.concatenate([i["L0_attn_Wq"], i["L0_attn_Wkv"]], axis=0)
    arrays = {
        "x": i["x"].reshape(TOKENS, DIM),
        "wqkv_t": wqkv.T,
        "wout_t": i["L0_attn_Wout"].T,
        "g1": i["L0_attn_g1"].reshape(CH, P).T,
        "g2": i["L0_attn_g2"],
        "ctx_t": i["ctx_1024"].transpose(2, 0, 1).reshape(DIM, BATCH * CTX),
        "xwq": i["L0_xattn_W_q"],
        "xwk_t": i["L0_xattn_W_k"].T,
        "xwv_t": i["L0_xattn_W_v"].T,
        "xwout_t": i["L0_xattn_W_out"].T,
        "biases": np.stack([i[f"L0_xattn_b_{w}"].reshape(CH, P).T for w in "qkv"], axis=1),
        "xbout": i["L0_xattn_b_out"],
        "wr_t": i["L0_ffn_w_router"].T,
        "w_v": i["L0_ffn_w_v"],
        "w_proj": i["L0_ffn_w_proj"],
    }
    nc = bacc.Bacc("TRN2", target_bir_lowering=False, num_devices=1)
    args, feed = {}, {}
    for name, a in arrays.items():
        a = np.ascontiguousarray(a)
        feed[f"in_{name}"] = a
        args[name] = nc.dram_tensor(f"in_{name}", a.shape, mybir.dt.from_np(a.dtype), kind="ExternalInput").ap()
    out = nc.dram_tensor("out_0", (TOKENS, DIM), F32, kind="ExternalOutput").ap()
    build(nc, out=out, **args)
    r = run_bass_kernel_spmd(nc, [feed], core_ids=[0])
    return r.results[0]["out_0"].reshape(BATCH, SEQ, DIM)
```

```python
from contextlib import ExitStack

import concourse.bass as bass
from concourse import mybir

F32 = mybir.dt.float32
F32R = mybir.dt.float32r
I32 = mybir.dt.int32
ACT = mybir.ActivationFunctionType
ALU = mybir.AluOpType
AX = mybir.AxisListType

P = 128
BATCH, SEQ, DIM = 2, 1024, 256
TOKENS = BATCH * SEQ
TILES = TOKENS // P
TPB = SEQ // P
CH = DIM // P
HEADS, DH = 16, 64
GROUPS = 4
HPG = HEADS // GROUPS
QKV = HEADS * DH + 2 * DH
NQ = 3
QB = QKV // NQ
HPB = QB // DH
CTX, CPAD = 77, 80
XH, XD = 16, 16
HK = XH * CPAD
HKC = HK // P
SB = 4 * CPAD
EXP, HID = 4, 1024
SORTED = TOKENS // P + EXP - 1
ROW = DIM + 1
EPS = 1e-5
SIM_SCALE = 16.0
NEG = -1e30
RING = 4
KV = TPB + 2
XS = 4
WB = 3

STAGES = [
    ("heads_out", 3, -1, 0.00), ("probs_turn", 0, -3, 0.02), ("probs_turn", 1, -3, 0.04),
    ("q_norm", 0, 1, 0.05), ("probs_turn", 2, -3, 0.06), ("z2_turn", 0, -2, 0.08),
    ("out_turn", 0, -1, 0.10), ("q_high", 0, 1, 0.11), ("out_turn", 1, -1, 0.12), ("q_low", 0, 1, 0.16),
    ("xattn_out", 0, -3, 0.18), ("norm_x", 0, 2, 0.22), ("heads_out", 0, 0, 0.26),
    ("out_proj", 0, -1, 0.28), ("z_turn", 0, 2, 0.34),
    ("scores", 0, -2, 0.36), ("q_turn", 0, 1, 0.38), ("x2_logits", 0, -3, 0.27),
    ("scores", 1, -2, 0.40), ("q_turn", 1, 1, 0.42), ("scores", 2, -2, 0.44), ("xa_norm", 0, -1, 0.45),
    ("q_turn", 2, 1, 0.46), ("scores", 3, -2, 0.48), ("q_turn", 3, 1, 0.50), ("heads_out", 1, 0, 0.51),
    ("q_turn", 4, 1, 0.54), ("x1_stats", 0, -1, 0.56), ("qkv", 0, 2, 0.58), ("probs_exp", 0, -2, 0.60),
    ("qkv", 1, 2, 0.62), ("probs_sum", 0, -2, 0.65), ("qkv", 2, 2, 0.66), ("z2_norm", 0, -1, 0.68),
    ("qkv_squares", 0, 2, 0.72), ("heads_out", 2, 0, 0.76), ("qkv_sums", 0, 2, 0.78),
    ("probs_norm", 0, -2, 0.70),
]
READER = {
    "z_turn": ["act"], "qkv": ["act"] * 3, "q_turn": ["act", "dve", "act", "dve", "act"],
    "heads_out": ["dve"] * 4, "out_turn": ["act"] * 2, "out_proj": ["dve"], "z2_turn": ["act"],
    "scores": ["dve"] * 4, "probs_turn": ["act", "dve", "act"], "xattn_out": ["dve"],
}
LN = 4
AHEAD = 3
LATER = {"pe": 0, "dve": 2, "act": 3, "pool": 3}
IDLE_POSITIONS = 8
MIN_POSITIONS = 8
FIRST_SLOT, LAST_SLOT = -2, TILES - 1 + 3


def plan_steps():
    steps, start = [], []
    for t in range(TILES):
        for g in range(GROUPS):
            start.append(len(steps))
            steps += [(t, g, j) for j in range(t % TPB + 1)]
    start.append(len(steps))
    return steps, start


def plan_side(start, freed):
    positions, side = [], []
    counts = {e: sum(1 for q, _ in freed if q == e) for e in ("act", "dve")}
    for slot in range(FIRST_SLOT, LAST_SLOT + 1):
        if 0 <= slot < TILES:
            own = range(start[GROUPS * slot], start[GROUPS * (slot + 1)])
            ks = []
            most = len(own) - AHEAD
            for n, k in enumerate(own[:most]):
                ks += [k] + [None] * (max(most, MIN_POSITIONS - AHEAD) * (n + 1) // most - len(ks) - 1)
            ks += own[most:]
        else:
            ks = [None] * IDLE_POSITIONS
        here = [[] for _ in ks]
        placed = []
        for name, part, shift, at in STAGES:
            n = int(at * len(ks))
            if name == "heads_out" and shift == 0 and 0 <= slot < TILES:
                n = max(n, ks.index(start[GROUPS * slot + part + 1] - 1) + 1)
            placed.append((n, at, name, part, slot + shift))
        for n, at, name, part, t in sorted(placed):
            if not 0 <= t < TILES:
                continue
            job = None
            if name in READER:
                e = READER[name][part]
                counts[e] += 1
                job = len(freed)
                freed.append((e, counts[e]))
            here[n].append((name, part, t, job))
        positions += ks
        side += here
    return positions, side


def build(nc, x, wqkv_t, wout_t, g1, g2, ctx_t, xwq, xwk_t, xwv_t, xwout_t, biases, xbout,
          wr_t, w_v, w_proj, out):
    steps, group_start = plan_steps()
    N_STEPS = len(steps)
    setup = [("kv", m) for m in range(4)]
    for b in range(BATCH):
        setup += [("g", b, c, n) for c in range(CH) for n in range(4)]
        setup += [("bias", b, n) for n in range(4)]
        setup += [("v", b, n) for n in range(HKC)]
    freed = []
    for s in setup:
        e = "dve" if s[0] == "kv" else "act"
        freed.append((e, 1 + sum(1 for q, _ in freed if q == e)))
    positions, side = plan_side(group_start, freed)
    group_end = {group_start[n + 1] - 1: n for n in range(len(group_start) - 1)}
    job_of = {(name, part, t): job for here in side for name, part, t, job in here}
    N_SIDE = len(freed)

    x_rows = x.rearrange("(t p) d -> p t d", p=P)

    with ExitStack() as keep:
        def sem(name):
            return keep.enter_context(nc.semaphore(name))

        def sb(ctx, name, shape, dt=F32):
            return ctx.enter_context(nc.sbuf_tensor(name, shape, dt))

        under = ExitStack()
        fz = sb(under, "fz", [P, DIM])
        fzh = sb(under, "fzh", [P, CH, P], F32R)
        fzl = sb(under, "fzl", [P, CH, P], F32R)
        gate = sb(under, "gate", [P, 2, HID])
        hT = sb(under, "hT", [P, HID // P, P])
        under.close()
        xall = sb(keep, "xall", [P, TILES, ROW])
        ident = sb(keep, "ident", [P, P])
        half = sb(keep, "half", [P, HEADS + 2])
        logits = sb(keep, "logits", [P, TILES, EXP])
        pos_i = sb(keep, "pos_i", [P, TILES], I32)
        expert_i = sb(keep, "expert_i", [P, SORTED + 1], I32)
        tri = sb(keep, "tri", [P, P])
        ones = sb(keep, "ones", [P, P])
        pad_row = sb(keep, "pad_row", [P, ROW])
        idnum = sb(keep, "idnum", [P, TILES], I32)

        early = ExitStack()
        wqkv = sb(early, "wqkv", [P, CH, QKV])
        wout = sb(early, "wout", [P, HEADS * DH // P, DIM])
        g1c = sb(early, "g1c", [P, CH])
        g2b = sb(early, "g2b", [P, DIM])
        boutb = sb(early, "boutb", [P, DIM])
        wrb = sb(early, "wrb", [P, EXP, DIM])
        G = [sb(early, f"G{b}", [P, CH, HK]) for b in range(BATCH)]
        BI = [sb(early, f"BI{b}", [P, HK], F32R) for b in range(BATCH)]
        VP = [sb(early, f"VP{b}", [P, HKC, DIM]) for b in range(BATCH)]
        pick = sb(early, "pick", [P, P], F32R)
        stat = sb(early, "stat", [P, TILES, 6])
        mv = sb(early, "mv", [P, TILES, 2])
        rin = sb(early, "rin", [P, TILES])
        rstd = sb(early, "rstd", [P, TILES])
        floor = sb(early, "floor", [P, HEADS + 2])
        rn = sb(early, "rn", [P, HEADS + 2])
        temp = ExitStack()
        wk = sb(temp, "wk", [P, CH, DIM])
        wv = sb(temp, "wv", [P, CH, DIM])
        wq2 = sb(temp, "wq2", [P, CH, DIM])
        wo2 = sb(temp, "wo2", [P, CH, DIM])
        ctxs = sb(temp, "ctxs", [P, CH, BATCH * CTX])
        bcol = sb(temp, "bcol", [P, 3, CH])
        bqb = sb(temp, "bqb", [P, CH, P])
        kvT = sb(temp, "kvT", [P, 4, BATCH, CPAD])
        own = sb(temp, "own", [P, 8, CPAD])
        kbd = sb(temp, "kbd", [P, CH, 8, CPAD])
        vbd = sb(temp, "vbd", [P, CH, 8, CPAD])
        braw = sb(temp, "braw", [P, HK])
        bhi = sb(temp, "bhi", [P, HK], F32R)
        blo = sb(temp, "blo", [P, HK])
        rowm = sb(temp, "rowm", [P, 2])
        temp.close()
        z = [sb(early, f"z{n}", [P, DIM]) for n in range(2)]
        zT = sb(early, "zT", [P, CH, P])
        sq = sb(early, "sq", [P, QKV])
        qraw = sb(early, "qraw", [P, QKV])
        ss = sb(early, "ss", [P, HEADS + 2])
        ssc = sb(early, "ssc", [P, HEADS + 2])
        qn = sb(early, "qn", [P, HEADS + 2, DH])
        qhl = sb(early, "qhl", [P, HEADS + 2, 2, DH], F32R)
        kdup = sb(early, "kdup", [P, 2, 2, DH])
        qT = [sb(early, f"qT{n}", [P, HEADS, P], F32R) for n in range(2)]
        kT = sb(early, "kT", [P, KV, 2, P], F32R)
        vhi = sb(early, "vhi", [P, KV, DH + 2], F32R)
        vlo = sb(early, "vlo", [P, KV, DH + 2], F32R)
        pr = sb(early, "pr", [P, RING, HPG * P])
        ph = sb(early, "ph", [P, RING, HPG * P], F32R)
        pl = sb(early, "pl", [P, RING, HPG * P], F32R)
        oT = sb(early, "oT", [P, 2, HPG * P])
        rl = sb(early, "rl", [P, HPG])
        on = [sb(early, f"on{n}", [P, HEADS * DH]) for n in range(2)]
        onT = sb(early, "onT", [P, HEADS * DH // P, P])
        st2 = sb(early, "st2", [P, 6])
        mv2 = sb(early, "mv2", [P, LN, 2])
        ri2 = sb(early, "ri2", [P, LN, 1])
        rs2 = sb(early, "rs2", [P, LN, 1])
        xa = sb(early, "xa", [P, DIM])
        xc = sb(early, "xc", [P, DIM])
        z2 = sb(early, "z2", [P, DIM])
        z2T = sb(early, "z2T", [P, CH, P])
        mx = sb(early, "mx", [P, XH])
        sc = sb(early, "sc", [P, XH, CPAD])
        sm = sb(early, "sm", [P, XH])
        rsm = sb(early, "rsm", [P, XH])
        pT = sb(early, "pT", [P, HKC, P])
        z3 = sb(early, "z3", [P, DIM])
        junk = sb(early, "junk", [P, DIM])
        early.close()

        late = ExitStack()
        raw = sb(late, "raw", [P, 2, 2 * HID])
        whi = sb(late, "whi", [P, EXP, CH, 2 * HID], F32R)
        wlo = sb(late, "wlo", [P, EXP, CH, 2 * HID], F32R)
        wps = sb(late, "wps", [P, EXP, HID // P, DIM])
        xs = sb(late, "xs", [P, XS, ROW])
        fst = sb(late, "fst", [P, 6])
        fmv = sb(late, "fmv", [P, 2])
        fri = sb(late, "fri", [P, 1])
        frs = sb(late, "frs", [P, 1])
        res = sb(late, "res", [P, 2, DIM])
        best = sb(late, "best", [P, TILES])
        eq = sb(late, "eq", [P, TILES, EXP])
        oh = sb(late, "oh", [P, TILES, EXP])
        left = sb(late, "left", [P, TILES])
        base = sb(late, "base", [P, TILES + 1, EXP])
        tot = sb(late, "tot", [P, TILES, EXP])
        cnt_i = sb(late, "cnt_i", [P, EXP], I32)
        cnt_s = sb(late, "cnt_s", [P, EXP], I32)
        cnt_f = sb(late, "cnt_f", [P, EXP])
        end = sb(late, "end", [P, EXP + 1])
        off = sb(late, "off", [P, EXP])
        rank = sb(late, "rank", [P, TILES, EXP])
        posf = sb(late, "posf", [P, TILES])
        tnum_i = sb(late, "tnum_i", [P, SORTED + 1], I32)
        tnum = sb(late, "tnum", [P, SORTED + 1])
        ecmp = sb(late, "ecmp", [P, SORTED + 1])
        late.close()

        S = [keep.enter_context(nc.psum_tensor(f"S{n}", [P, 512], F32)) for n in range(AHEAD)]
        O = [keep.enter_context(nc.psum_tensor(f"O{n}", [P, 512], F32)) for n in range(2)]
        W = [keep.enter_context(nc.psum_tensor(f"W{n}", [P, 512], F32)) for n in range(WB)]

        HT = [W[2], S[2]]

        sorted_rows = nc.dram_tensor("sorted_rows", [SORTED * P, ROW], F32, kind="Internal").ap()

        x_in = [sem(f"x_in{b}") for b in range(BATCH)]
        w_in = sem("w_in")
        wk_in = sem("wk_in")
        wo_in = sem("wo_in")
        rows_in = sem("rows_in")
        consts = sem("consts")
        spread = sem("spread")
        dconst = sem("dconst")
        wq_scaled = sem("wq_scaled")
        side_ready = sem("side_ready")
        act_freed = sem("act_freed")
        dve_freed = sem("dve_freed")
        own_ok = sem("own_ok")
        bd_ready = sem("bd_ready")
        bd_used = sem("bd_used")
        braw_ready = sem("braw_ready")
        bias_step = sem("bias_step")
        stats_ok = sem("stats_ok")
        stats_in = sem("stats_in")
        rstd_ok = sem("rstd_ok")
        z_ready = sem("z_ready")
        sq_ready = sem("sq_ready")
        ss_ready = sem("ss_ready")
        ssc_ready = sem("ssc_ready")
        rn_ready = sem("rn_ready")
        qhi_ready = sem("qhi_ready")
        qlo_ready = sem("qlo_ready")
        kdup_ready = sem("kdup_ready")
        v_ready = sem("v_ready")
        s_ready = sem("s_ready")
        p_ready = sem("p_ready")
        masked = sem("masked")
        ph_ready = sem("ph_ready")
        pl_ready = sem("pl_ready")
        pv_done = sem("pv_done")
        ot_ready = sem("ot_ready")
        rl_ready = sem("rl_ready")
        on_ready = sem("on_ready")
        ln_step = sem("ln_step")
        ln_root = sem("ln_root")
        qn_ready = sem("qn_ready")
        ln_self = sem("ln_self")
        xa_ready = sem("xa_ready")
        x1_ready = sem("x1_ready")
        xa_step = sem("xa_step")
        z2_ready = sem("z2_ready")
        x1b_ready = sem("x1b_ready")
        mx_ready = sem("mx_ready")
        sc_ready = sem("sc_ready")
        pe_ready = sem("pe_ready")
        sm_ready = sem("sm_ready")
        rsm_ready = sem("rsm_ready")
        pn_ready = sem("pn_ready")
        x2_ready = sem("x2_ready")
        z3_ready = sem("z3_ready")
        logit_ready = sem("logit_ready")
        act_done = sem("act_done")
        pe_done = sem("pe_done")
        route = sem("route")
        counted = sem("counted")
        pos_ready = sem("pos_ready")
        pad_out = sem("pad_out")
        scattered = sem("scattered")
        ffn_w = sem("ffn_w")
        tile_num = sem("tile_num")
        xs_in = [sem(f"xs_in{n}") for n in range(XS)]
        raw_in = [sem(f"raw_in{n}") for n in range(2)]
        whi_ready = sem("whi_ready")
        wlo_ready = sem("wlo_ready")
        fzh_ready = sem("fzh_ready")
        f_self = sem("f_self")
        f_root = sem("f_root")
        f_step = sem("f_step")
        fz_ready = sem("fz_ready")
        f_turn = sem("f_turn")
        fzT_ready = sem("fzT_ready")
        up_ready = sem("up_ready")
        gate_ready = sem("gate_ready")
        h_ready = sem("h_ready")
        h_turned = sem("h_turned")
        hT_ready = sem("hT_ready")
        down_ready = sem("down_ready")
        res_ready = sem("res_ready")
        stored = [sem(f"stored{n}") for n in range(2)]

        block = keep.enter_context(nc.Block())

        def freed_wait(eng, job):
            if job >= WB:
                who, n = freed[job - WB]
                eng.wait_ge(act_freed if who == "act" else dve_freed, n)

        def store(pool, n):
            pool.wait_ge(res_ready, n + 1)
            pool.indirect_dma_start(out=out, out_offset=bass.IndirectOffsetOnAxis(
                ap=xs[:, n % XS, DIM:ROW].bitcast(I32), axis=0), in_=res[:, n % 2, :], in_offset=None,
                bounds_check=TOKENS - 1, oob_is_err=False).then_inc(stored[n % 2], 16)

        def program(engine):
            for n in range(len(positions) + LATER[engine]):
                k = positions[n] if n < len(positions) else None
                m = n - LATER[engine]
                yield k, side[m] if m >= 0 else []

        def freed_count(name, part, t):
            return freed[job_of[name, part, t]][1]

        def job_count(name, part, t):
            return job_of[name, part, t] + 1

        @block.sync
        def _(sp):
            for b in range(BATCH):
                sp.dma_start(xall[:, b * TPB:(b + 1) * TPB, 0:DIM], x_rows[:, b * TPB:(b + 1) * TPB, :])\
                    .then_inc(x_in[b], 16)
            sp.dma_start(wk[:], xwk_t.rearrange("(c p) n -> p c n", p=P)).then_inc(wk_in, 16)
            sp.dma_start(wv[:], xwv_t.rearrange("(c p) n -> p c n", p=P)).then_inc(wk_in, 16)
            sp.dma_start(ctxs[:], ctx_t.rearrange("(c p) n -> p c n", p=P)).then_inc(wk_in, 16)
            sp.dma_start(bcol[:], biases).then_inc(wk_in, 16)
            sp.dma_start(wq2[:], xwq.rearrange("(c p) n -> p c n", p=P)).then_inc(wk_in, 16)
            sp.dma_start(wo2[:], xwout_t.rearrange("(c p) n -> p c n", p=P)).then_inc(wk_in, 16)
            sp.dma_start(wout[:], wout_t.rearrange("(c p) n -> p c n", p=P)).then_inc(wo_in, 16)
            sp.wait_ge(consts, 14)
            for n in range(SORTED):
                sp.dma_start(sorted_rows[n * P:(n + 1) * P, :], pad_row[:]).then_inc(pad_out, 16)
            sp.wait_ge(logit_ready, TILES)
            sp.wait_ge(act_done, 1)
            sp.wait_ge(pe_done, 1)
            for n in range(EXP * CH):
                e, c = n // CH, n % CH
                if n >= 2:
                    sp.wait_ge(wlo_ready, n - 1)
                sp.dma_start(raw[:, n % 2, :], w_v[e, c * P:(c + 1) * P, :]).then_inc(raw_in[n % 2], 16)
                if c == 0:
                    sp.dma_start(wps[:, e], w_proj[e].rearrange("(c p) n -> p c n", p=P)).then_inc(ffn_w, 16)
            sp.wait_ge(scattered, 16 * TILES)
            for n in range(SORTED):
                if n >= XS:
                    sp.wait_ge(stored[(n - XS) % 2], 16 * ((n - XS) // 2 + 1))
                sp.dma_start(xs[:, n % XS, :], sorted_rows[n * P:(n + 1) * P, :]).then_inc(xs_in[n % XS], 16)

        @block.gpsimd
        def _(pool):
            nc.gpsimd.memset(ident[:], 0.0).then_inc(consts, 1)
            nc.gpsimd.memset(tri[:], 1.0).then_inc(consts, 1)
            nc.gpsimd.memset(own[:], 1.0).then_inc(consts, 1)
            nc.gpsimd.memset(rowm[:], 0.0).then_inc(consts, 1)
            nc.gpsimd.memset(half[:], -0.5).then_inc(consts, 1)
            nc.gpsimd.memset(ones[:], 1.0).then_inc(consts, 1)
            nc.gpsimd.memset(pad_row[:], 0.0).then_inc(consts, 1)
            nc.gpsimd.memset(g2b[0:1, 0:1], 0.0).then_inc(consts, 1)
            pool.wait_ge(consts, 8)
            nc.gpsimd.affine_select(out=ident[:], in_=ident[:], compare_op=ALU.not_equal, fill=1.0, base=0,
                                    pattern=[[-1, P]], channel_multiplier=1).then_inc(consts, 1)
            nc.gpsimd.affine_select(out=tri[:], in_=tri[:], compare_op=ALU.is_gt, fill=0.0, base=0,
                                    pattern=[[1, P]], channel_multiplier=-1).then_inc(consts, 1)
            nc.gpsimd.affine_select(out=own[:], in_=own[:], compare_op=ALU.is_ge, fill=0.0, base=0,
                                    pattern=[[-XD, 8], [0, CPAD]], channel_multiplier=1).then_inc(own_ok, 1)
            for n in range(2):
                nc.gpsimd.affine_select(out=rowm[:, n:n + 1], in_=rowm[:, n:n + 1], compare_op=ALU.not_equal,
                                        fill=1.0, base=-n, pattern=[[0, 1]], channel_multiplier=1).then_inc(consts, 1)
            pool.wait_ge(own_ok, 1)
            nc.gpsimd.affine_select(out=own[:], in_=own[:], compare_op=ALU.is_ge, fill=0.0, base=XD - 1,
                                    pattern=[[XD, 8], [0, CPAD]], channel_multiplier=-1).then_inc(own_ok, 1)
            nc.gpsimd.iota(xall[:, :, DIM:ROW].bitcast(I32), pattern=[[P, TILES], [0, 1]], base=0,
                           channel_multiplier=1).then_inc(consts, 1)
            nc.gpsimd.iota(pad_row[:, DIM:ROW].bitcast(I32), pattern=[[0, 1]], base=TOKENS,
                           channel_multiplier=0).then_inc(consts, 1)
            pool.dma_start(g2b[0:1, :], g2.rearrange("(a n) -> a n", a=1)).then_inc(rows_in, 16)
            pool.dma_start(boutb[0:1, :], xbout.rearrange("(a n) -> a n", a=1)).then_inc(rows_in, 16)
            pool.dma_start(wrb[0:1, :, :], wr_t.rearrange("(a e) n -> a e n", a=1)).then_inc(rows_in, 16)
            pool.wait_ge(consts, 14)
            pool.wait_ge(rows_in, 48)
            nc.gpsimd.partition_broadcast(g2b[:], g2b[0:1, :]).then_inc(spread, 1)
            nc.gpsimd.partition_broadcast(boutb[:], boutb[0:1, :]).then_inc(spread, 1)
            nc.gpsimd.partition_broadcast(wrb[:].rearrange("p e n -> p (e n)"),
                                          wrb[0:1].rearrange("p e n -> p (e n)")).then_inc(spread, 1)
            pool.wait_ge(stats_in, 1)
            nc.gpsimd.tensor_tensor(rstd[:], rin[:], half[:, 0:TILES], ALU.pow).then_inc(rstd_ok, 1)

            n_root = 0

            def root():
                nonlocal n_root
                n_root += 1
                pool.wait_ge(ln_step, n_root)
                if n_root > LN:
                    pool.wait_ge(ln_step, n_root)
                nc.gpsimd.tensor_tensor(rs2[:, n_root % LN, :], ri2[:, n_root % LN, :], half[:, 0:1], ALU.pow).then_inc(ln_root, 1)

            for k, stages in program("pool"):
                if k is not None and steps[k][2] == steps[k][0] % TPB:
                    pool.wait_ge(p_ready, k + 1)
                    blk = pr[:, k % RING, :].rearrange("p (h q) -> p h q", h=HPG)
                    nc.gpsimd.affine_select(out=blk, in_=blk, compare_op=ALU.is_ge, fill=0.0, base=0,
                                            pattern=[[0, HPG], [1, P]], channel_multiplier=-1).then_inc(masked, 1)
                for name, part, t, job in stages:
                    if name == "qkv_sums":
                        pool.wait_ge(ssc_ready, t + 1)
                        if t >= 1:
                            pool.wait_ge(qn_ready, t)
                        nc.gpsimd.tensor_tensor(rn[:, 0:HEADS + 1], ssc[:, 0:HEADS + 1], half[:, 0:HEADS + 1],
                                                ALU.pow).then_inc(rn_ready, 1)
                    elif name == "q_low":
                        pool.wait_ge(qhi_ready, t + 1)
                        pool.wait_ge(qlo_ready, t + 1)
                        if t >= KV:
                            pool.wait_ge(pv_done, group_start[GROUPS * TPB * ((t - KV) // TPB + 1)])
                        vs = t % KV
                        nc.gpsimd.tensor_copy(vhi[:, vs, 0:DH], qhl[:, HEADS + 1, 0, :].bitcast(F32)).then_inc(v_ready, 1)
                        nc.gpsimd.tensor_copy(vlo[:, vs, 0:DH], qhl[:, HEADS + 1, 1, :].bitcast(F32)).then_inc(v_ready, 1)
                    elif name == "out_proj":
                        root()
                    elif name == "xa_norm":
                        pool.wait_ge(xa_ready, t + 1)
                        nc.gpsimd.tensor_tensor(xa[:], xa[:], g2b[:], ALU.mult).then_inc(xa_step, 1)
                        pool.wait_ge(xa_step, t + 1)
                        nc.gpsimd.tensor_tensor(xall[:, t, 0:DIM], xall[:, t, 0:DIM], xa[:], ALU.add)\
                            .then_inc(x1_ready, 1)
                    elif name == "x1_stats":
                        root()
                    elif name == "z2_norm":
                        pool.wait_ge(z2_ready, t + 1)
                        nc.gpsimd.tensor_tensor(xall[:, t, 0:DIM], xall[:, t, 0:DIM], boutb[:], ALU.add)\
                            .then_inc(x1b_ready, 1)
                    elif name == "probs_norm":
                        pool.wait_ge(rsm_ready, t + 1)
                        nc.gpsimd.tensor_tensor(sc[:], sc[:], rsm[:].unsqueeze(2).broadcast_to([P, XH, CPAD]),
                                                ALU.mult).then_inc(pn_ready, 1)
                    elif name == "xattn_out":
                        root()

            pool.wait_ge(pad_out, 16 * SORTED)
            pool.wait_ge(x2_ready, TILES)
            pool.wait_ge(logit_ready, TILES)
            nc.gpsimd.iota(tnum_i[:], pattern=[[1, SORTED + 1]], base=0, channel_multiplier=0).then_inc(tile_num, 1)
            pool.wait_ge(pos_ready, 1)
            for t in range(TILES):
                pool.indirect_dma_start(out=sorted_rows, out_offset=bass.IndirectOffsetOnAxis(ap=pos_i[:, t:t + 1], axis=0),
                                        in_=xall[:, t, :], in_offset=None).then_inc(scattered, 16)
            for n in range(SORTED):
                pool.wait_ge(f_step, n + 1)
                nc.gpsimd.tensor_tensor(frs[:], fri[:], half[:, 0:1], ALU.pow).then_inc(f_root, 1)
                if n >= 2:
                    store(pool, n - 2)
            store(pool, SORTED - 2)
            store(pool, SORTED - 1)
            for n in range(2):
                pool.wait_ge(stored[n], 16 * ((SORTED - n + 1) // 2))

        @block.scalar
        def _(act):
            def carry_off(G_):
                act.wait_ge(pv_done, group_start[G_ + 1])
                if G_ >= 2:
                    act.wait_ge(rl_ready, G_ - 1)
                nc.scalar.copy(oT[0:DH + 1, G_ % 2, :], O[G_ % 2][0:DH + 1, :]).then_inc(ot_ready, 1)

            act.dma_start(wqkv[:], wqkv_t.rearrange("(c p) n -> p c n", p=P)).then_inc(w_in, 16)
            act.dma_start(g1c[:], g1).then_inc(w_in, 16)
            for job, s in enumerate(setup):
                if s[0] == "kv":
                    continue
                act.wait_ge(side_ready, job + 1)
                w = W[job % WB]
                if s[0] == "g":
                    _, b, c, n = s
                    nc.scalar.copy(G[b][:, c, n * SB:(n + 1) * SB], w[:, 0:SB]).then_inc(act_freed, 1)
                elif s[0] == "bias":
                    _, b, n = s
                    if b > 0 and n == 0:
                        act.wait_ge(bias_step, 5 * b)
                    nc.scalar.copy(braw[:, n * SB:(n + 1) * SB], w[:, 0:SB]).then_inc(act_freed, 1)
                else:
                    _, b, n = s
                    nc.scalar.copy(VP[b][:, n, :], w[:, 0:DIM]).then_inc(act_freed, 1)

            for n, (k, stages) in enumerate(program("act")):
                if k is not None:
                    act.wait_ge(s_ready, k + 1)
                    if k >= RING:
                        act.wait_ge(pl_ready, k - RING + 1)
                    nc.scalar.activation(pr[:, k % RING, :], S[k % AHEAD][:], ACT.Exp, scale=SIM_SCALE)\
                        .then_inc(p_ready, 1)
                if 0 <= n - AHEAD < len(positions) and positions[n - AHEAD] in group_end:
                    carry_off(group_end[positions[n - AHEAD]])
                for name, part, t, job in stages:
                    if name == "z_turn":
                        act.wait_ge(side_ready, job + 1)
                        if t >= 1:
                            act.wait_ge(side_ready, job_count("qkv", 2, t - 1))
                        nc.scalar.copy(zT[:].rearrange("p c n -> p (c n)"), W[job % WB][:, 0:DIM]).then_inc(act_freed, 1)
                    elif name == "qkv":
                        act.wait_ge(side_ready, job + 1)
                        if t >= 1 and part == 0:
                            act.wait_ge(qn_ready, t)
                            act.wait_ge(sq_ready, t)
                        nc.scalar.copy(qraw[:, part * QB:(part + 1) * QB], W[job % WB][:, 0:QB]).then_inc(act_freed, 1)
                    elif name == "qkv_squares":
                        act.wait_ge(act_freed, freed_count("qkv", 2, t))
                        if t >= 1:
                            act.wait_ge(ss_ready, t)
                        nc.scalar.activation(sq[:], qraw[:], ACT.Square).then_inc(sq_ready, 1)
                    elif name == "q_high":
                        act.wait_ge(qn_ready, t + 1)
                        if t >= 1:
                            act.wait_ge(side_ready, job_count("q_turn", 4, t - 1))
                            act.wait_ge(v_ready, 2 * t)
                            act.wait_ge(kdup_ready, 2 * t)
                        nc.scalar.copy(qhl[:, :, 0, :], qn[:]).then_inc(qhi_ready, 1)
                    elif name == "q_turn" and part in (0, 2):
                        act.wait_ge(side_ready, job + 1)
                        if t >= 2:
                            act.wait_ge(s_ready, group_start[GROUPS * (t - 1)])
                        nc.scalar.copy(qT[t % 2][:, 4 * part:4 * part + 4, :].rearrange("p h q -> p (h q)"),
                                       W[job % WB][:]).then_inc(act_freed, 1)
                    elif name == "q_turn" and part == 4:
                        act.wait_ge(side_ready, job + 1)
                        if t >= KV:
                            act.wait_ge(s_ready, group_start[GROUPS * TPB * ((t - KV) // TPB + 1)])
                        nc.scalar.copy(kT[:, t % KV].rearrange("p a k -> p (a k)"), W[job % WB][:, 0:2 * P])\
                            .then_inc(act_freed, 1)
                    elif name == "out_turn":
                        act.wait_ge(side_ready, job + 1)
                        if t >= 1 and part == 0:
                            act.wait_ge(side_ready, job_count("out_proj", 0, t - 1))
                        nc.scalar.copy(onT[:, 4 * part:4 * part + 4, :].rearrange("p c q -> p (c q)"), W[job % WB][:])\
                            .then_inc(act_freed, 1)
                    elif name == "z2_turn":
                        act.wait_ge(side_ready, job + 1)
                        if t >= 1:
                            act.wait_ge(side_ready, job_count("scores", 3, t - 1))
                        nc.scalar.copy(z2T[:].rearrange("p c n -> p (c n)"), W[job % WB][:, 0:DIM]).then_inc(act_freed, 1)
                    elif name == "probs_exp":
                        act.wait_ge(sc_ready, t + 1)
                        nc.scalar.activation(sc[:], sc[:], ACT.Exp).then_inc(pe_ready, 1)
                    elif name == "probs_turn" and part != 1:
                        act.wait_ge(side_ready, job + 1)
                        if t >= 1 and part == 0:
                            act.wait_ge(side_ready, job_count("xattn_out", 0, t - 1))
                        c = min(4, HKC - 4 * part)
                        nc.scalar.copy(pT[:, 4 * part:4 * part + c, :].rearrange("p c q -> p (c q)"),
                                       W[job % WB][:, 0:c * P]).then_inc(act_freed, 1)
            act.wait_ge(act_freed, max(n for e, n in freed if e == "act"))
            act.wait_ge(pe_ready, TILES)
            act.wait_ge(qhi_ready, TILES)
            act.sem_inc(act_done, 1)

            for n in range(EXP * CH):
                act.wait_ge(raw_in[n % 2], 16 * (n // 2 + 1))
                nc.scalar.copy(whi[:, n // CH, n % CH, :], raw[:, n % 2, :]).then_inc(whi_ready, 1)

            def rows_high(n):
                act.wait_ge(f_turn, n + 1)
                if n >= 1:
                    act.wait_ge(up_ready, 2 * n)
                nc.scalar.copy(fzh[:].rearrange("p c n -> p (c n)"), W[0][:, 0:DIM]).then_inc(fzh_ready, 1)

            def hidden_out(n):
                for c in range(2):
                    act.wait_ge(h_turned, 2 * n + c + 1)
                    if n >= 1 and c == 0:
                        act.wait_ge(down_ready, n)
                    nc.scalar.copy(hT[:, 4 * c:4 * c + 4, :].rearrange("p c q -> p (c q)"), HT[c][:]).then_inc(hT_ready, 1)

            rows_high(0)
            for n in range(SORTED):
                act.wait_ge(up_ready, 2 * n + 1)
                if n >= 2:
                    act.wait_ge(h_turned, 2 * (n - 1))
                for c in range(2):
                    nc.scalar.activation(gate[:, n % 2, c * 512:(c + 1) * 512], S[c][:], ACT.Silu).then_inc(gate_ready, 1)
                if n + 1 < SORTED:
                    rows_high(n + 1)
                if n >= 1:
                    hidden_out(n - 1)
            hidden_out(SORTED - 1)

        @block.vector
        def _(dve):
            n_ln = 0
            n_used = 0
            n_self = 0

            def own_step(ins):
                nonlocal n_self
                n_self += 1
                ins.then_inc(ln_self, 1)
                dve.wait_ge(ln_self, n_self)

            def root_of(src):
                nonlocal n_ln
                n_ln += 1
                n = n_ln % LN
                own_step(nc.vector.bn_stats(st2[:], src))
                own_step(nc.vector.bn_aggr(mv2[:, n, :], st2[:]))
                if n_ln > LN:
                    dve.wait_ge(ln_root, n_ln - LN)
                nc.vector.tensor_scalar(ri2[:, n, :], mv2[:, n, 1:2], EPS, None, ALU.add).then_inc(ln_step, 1)

            def normed(out_, src):
                nonlocal n_used
                n_used += 1
                dve.wait_ge(ln_root, n_used)
                return nc.vector.tensor_scalar(out_, src, mv2[:, n_used % LN, 0:1], rs2[:, n_used % LN, :],
                                               ALU.subtract, ALU.mult)

            nc.vector.memset(floor[:, 0:HEADS], 3.90625e-27).then_inc(dconst, 1)
            nc.vector.memset(floor[:, HEADS:HEADS + 2], 1e-24).then_inc(dconst, 1)
            nc.vector.memset(rn[:], 1.0).then_inc(dconst, 1)
            nc.vector.memset(kvT[:], 0.0).then_inc(dconst, 1)
            nc.vector.memset(braw[:], 0.0).then_inc(dconst, 1)
            dve.wait_ge(dconst, 5)

            for t in range(TILES):
                dve.wait_ge(x_in[t // TPB], 16)
                nc.vector.bn_stats(stat[:, t, :], xall[:, t, 0:DIM]).then_inc(stats_ok, 1)
            for t in range(TILES):
                dve.wait_ge(stats_ok, t + 1)
                nc.vector.bn_aggr(mv[:, t, :], stat[:, t, :]).then_inc(stats_ok, 1)
            dve.wait_ge(stats_ok, 2 * TILES)
            nc.vector.tensor_scalar(rin[:], mv[:, :, 1], 1.0 + EPS, EPS * EPS, ALU.mult, ALU.add).then_inc(stats_in, 1)
            dve.wait_ge(w_in, 32)
            for c in range(CH):
                nc.vector.tensor_scalar(wqkv[:, c, :], wqkv[:, c, :], g1c[:, c:c + 1], None, ALU.mult).then_inc(wq_scaled, 1)

            dve.wait_ge(wk_in, 16 * 6)
            for m in range(CH):
                nc.vector.tensor_copy(bqb[:, m, :], bcol[:, 0, m:m + 1].broadcast_to([P, P])).then_inc(bd_ready, 1)
            for m in range(4):
                dve.wait_ge(side_ready, m + 1)
                src = W[m % WB][:, 0:BATCH * CTX].rearrange("p (b k) -> p b k", b=BATCH)
                nc.vector.tensor_scalar(kvT[:, m, :, 0:CTX], src, bcol[:, 1 + m // CH, m % CH:m % CH + 1],
                                        0.25 if m < CH else 1.0, ALU.add, ALU.mult).then_inc(dve_freed, 1)
            dve.wait_ge(dve_freed, 4)
            dve.wait_ge(own_ok, 2)
            dve.wait_ge(consts, 14)
            for b in range(BATCH):
                if b > 0:
                    dve.wait_ge(side_ready, 4 + 22 * b)
                for m in range(CH):
                    for dst, src in ((kbd, m), (vbd, CH + m)):
                        nc.vector.tensor_tensor(dst[:, m], own[:], kvT[:, src, b, :].unsqueeze(1).broadcast_to([P, 8, CPAD]),
                                                ALU.mult).then_inc(bd_ready, 1)
                dve.wait_ge(act_freed, 22 * b + 12)
                pads = braw[:].rearrange("p (h k) -> p h k", k=CPAD)[:, :, CTX:CPAD]
                nc.vector.memset(pads, NEG).then_inc(bias_step, 1)
                dve.wait_ge(bias_step, 5 * b + 1)
                nc.vector.tensor_copy(bhi[:], braw[:]).then_inc(bias_step, 1)
                dve.wait_ge(bias_step, 5 * b + 2)
                nc.vector.tensor_tensor(blo[:], braw[:], bhi[:].bitcast(F32), ALU.subtract).then_inc(bias_step, 1)
                dve.wait_ge(bias_step, 5 * b + 3)
                nc.vector.tensor_scalar(blo[:], blo[:], rowm[:, 1:2], None, ALU.mult).then_inc(bias_step, 1)
                dve.wait_ge(bias_step, 5 * b + 4)
                nc.vector.scalar_tensor_tensor(out=BI[b][:], in0=bhi[:].bitcast(F32), scalar=rowm[:, 0:1], in1=blo[:],
                                               op0=ALU.mult, op1=ALU.add).then_inc(bias_step, 1)
            nc.vector.tensor_scalar(pick[:], ones[:], rowm[:, 0:1], rowm[:, 1:2], ALU.mult, ALU.add).then_inc(bias_step, 1)
            dve.wait_ge(bias_step, 5 * BATCH + 1)

            dve.wait_ge(side_ready, len(setup))
            dve.wait_ge(act_freed, len(setup) - 4)
            nc.vector.memset(vhi[:, :, DH:DH + 2].bitcast(F32), 1.0).then_inc(dconst, 1)
            nc.vector.memset(vlo[:, :, DH:DH + 2].bitcast(F32), 0.0).then_inc(dconst, 1)
            dve.wait_ge(rstd_ok, 1)

            diag = 0
            for k, stages in program("dve"):
                if k is not None:
                    t, _, j = steps[k]
                    if j == t % TPB:
                        diag += 1
                        dve.wait_ge(masked, diag)
                    else:
                        dve.wait_ge(p_ready, k + 1)
                    if k >= RING:
                        dve.wait_ge(pv_done, k - RING + 1)
                    nc.vector.tensor_copy(ph[:, k % RING, :], pr[:, k % RING, :]).then_inc(ph_ready, 1)
                    dve.wait_ge(ph_ready, k + 1)
                    nc.vector.tensor_tensor(pl[:, k % RING, :], pr[:, k % RING, :], ph[:, k % RING, :].bitcast(F32),
                                            ALU.subtract).then_inc(pl_ready, 1)
                for name, part, t, job in stages:
                    if name == "norm_x":
                        if t >= 2:
                            dve.wait_ge(side_ready, job_count("z_turn", 0, t - 2))
                        nc.vector.tensor_scalar(z[t % 2][:], xall[:, t, 0:DIM], mv[:, t, 0:1], rstd[:, t:t + 1],
                                                ALU.subtract, ALU.mult).then_inc(z_ready, 1)
                    elif name == "qkv_sums":
                        dve.wait_ge(sq_ready, t + 1)
                        if t >= 1:
                            dve.wait_ge(ssc_ready, t)
                        nc.vector.tensor_reduce(ss[:], sq[:].rearrange("p (h d) -> p h d", d=DH), AX.X, ALU.add)\
                            .then_inc(ss_ready, 1)
                        dve.wait_ge(ss_ready, t + 1)
                        if t >= 1:
                            dve.wait_ge(rn_ready, t)
                        nc.vector.tensor_tensor(ssc[:], ss[:], floor[:], ALU.max).then_inc(ssc_ready, 1)
                    elif name == "q_norm":
                        dve.wait_ge(rn_ready, t + 1)
                        if t >= 1:
                            dve.wait_ge(qhi_ready, t)
                            dve.wait_ge(qlo_ready, t)
                        nc.vector.tensor_tensor(qn[:], qraw[:].rearrange("p (h d) -> p h d", d=DH),
                                                rn[:].unsqueeze(2).broadcast_to([P, HEADS + 2, DH]), ALU.mult)\
                            .then_inc(qn_ready, 1)
                    elif name == "q_low":
                        dve.wait_ge(qhi_ready, t + 1)
                        nc.vector.tensor_tensor(qhl[:, :, 1, :], qn[:], qhl[:, :, 0, :].bitcast(F32), ALU.subtract)\
                            .then_inc(qlo_ready, 1)
                        dve.wait_ge(qlo_ready, t + 1)
                        for n in range(2):
                            nc.vector.tensor_copy(kdup[:, n], qhl[:, HEADS, n, :].bitcast(F32).unsqueeze(1).broadcast_to([P, 2, DH]))\
                                .then_inc(kdup_ready, 1)
                    elif name == "q_turn" and part in (1, 3):
                        dve.wait_ge(side_ready, job + 1)
                        if t >= 2:
                            dve.wait_ge(s_ready, group_start[GROUPS * (t - 1)])
                        nc.vector.tensor_copy(qT[t % 2][:, 4 * part:4 * part + 4, :].rearrange("p h q -> p (h q)"),
                                              W[job % WB][:]).then_inc(dve_freed, 1)
                    elif name == "probs_turn" and part == 1:
                        dve.wait_ge(side_ready, job + 1)
                        nc.vector.tensor_copy(pT[:, 4:8, :].rearrange("p c q -> p (c q)"), W[job % WB][:]).then_inc(dve_freed, 1)
                    elif name == "heads_out":
                        dve.wait_ge(side_ready, job + 1)
                        src = W[job % WB][:, 0:HPG * (DH + 1)].rearrange("p (h d) -> p h d", d=DH + 1)
                        if part > 0 or t > 0:
                            dve.wait_ge(dve_freed, freed_count("heads_out", (part - 1) % GROUPS, t if part else t - 1))
                        nc.vector.reciprocal(rl[:], src[:, :, DH]).then_inc(rl_ready, 1)
                        dve.wait_ge(rl_ready, GROUPS * t + part + 1)
                        if t >= 2 and part == 0:
                            dve.wait_ge(side_ready, job_count("out_turn", 1, t - 2))
                        nc.vector.tensor_tensor(
                            on[t % 2][:, part * DIM:(part + 1) * DIM].rearrange("p (h d) -> p h d", d=DH),
                            src[:, :, 0:DH], rl[:].unsqueeze(2).broadcast_to([P, HPG, DH]), ALU.mult)\
                            .then_inc(dve_freed, 1)
                    elif name == "out_proj":
                        dve.wait_ge(side_ready, job + 1)
                        if t >= 1:
                            dve.wait_ge(xa_ready, t)
                        nc.vector.tensor_copy(xc[:], W[job % WB][:, 0:DIM]).then_inc(dve_freed, 1)
                        dve.wait_ge(dve_freed, freed[job][1])
                        root_of(xc[:])
                    elif name == "xa_norm":
                        if t >= 1:
                            dve.wait_ge(x1_ready, t)
                        normed(xa[:], xc[:]).then_inc(xa_ready, 1)
                    elif name == "x1_stats":
                        dve.wait_ge(x1_ready, t + 1)
                        root_of(xall[:, t, 0:DIM])
                    elif name == "z2_norm":
                        if t >= 1:
                            dve.wait_ge(side_ready, job_count("z2_turn", 0, t - 1))
                        normed(z2[:], xall[:, t, 0:DIM]).then_inc(z2_ready, 1)
                    elif name == "scores":
                        dve.wait_ge(side_ready, job + 1)
                        if t >= 1 and part == 0:
                            dve.wait_ge(side_ready, job_count("probs_turn", 2, t - 1))
                        src = W[job % WB][:, 0:SB].rearrange("p (h k) -> p h k", k=CPAD)
                        nc.vector.tensor_reduce(mx[:, 4 * part:4 * part + 4], src, AX.X, ALU.max).then_inc(mx_ready, 1)
                        dve.wait_ge(mx_ready, 4 * t + part + 1)
                        nc.vector.tensor_tensor(sc[:, 4 * part:4 * part + 4, :], src,
                                                mx[:, 4 * part:4 * part + 4].unsqueeze(2).broadcast_to([P, 4, CPAD]),
                                                ALU.subtract).then_inc(dve_freed, 1)
                        if part == 3:
                            dve.wait_ge(dve_freed, freed[job][1])
                            dve.sem_inc(sc_ready, 1)
                    elif name == "probs_sum":
                        dve.wait_ge(pe_ready, t + 1)
                        nc.vector.tensor_reduce(sm[:], sc[:], AX.X, ALU.add).then_inc(sm_ready, 1)
                        dve.wait_ge(sm_ready, t + 1)
                        if t >= 1:
                            dve.wait_ge(pn_ready, t)
                        nc.vector.reciprocal(rsm[:], sm[:]).then_inc(rsm_ready, 1)
                    elif name == "xattn_out":
                        dve.wait_ge(side_ready, job + 1)
                        dve.wait_ge(x1b_ready, t + 1)
                        nc.vector.tensor_tensor(xall[:, t, 0:DIM], xall[:, t, 0:DIM], W[job % WB][:, 0:DIM], ALU.add)\
                            .then_inc(dve_freed, 1)
                        dve.wait_ge(dve_freed, freed[job][1])
                        dve.sem_inc(x2_ready, 1)
                        root_of(xall[:, t, 0:DIM])
                    elif name == "x2_logits":
                        normed(z3[:], xall[:, t, 0:DIM]).then_inc(z3_ready, 1)
                        dve.wait_ge(z3_ready, t + 1)
                        for e in range(EXP):
                            last = nc.vector.tensor_tensor_reduce(junk[:], z3[:], wrb[:, e, :], 1.0, 0.0, ALU.mult, ALU.add,
                                                                  logits[:, t, e:e + 1])
                            own_step(last)
                        dve.sem_inc(logit_ready, 1)

            n_r = 0

            def r(ins):
                nonlocal n_r
                n_r += 1
                ins.then_inc(route, 1)
                dve.wait_ge(route, n_r)

            dve.wait_ge(act_done, 1)
            dve.wait_ge(pe_done, 1)
            r(nc.vector.tensor_reduce(best[:], logits[:], AX.X, ALU.max))
            r(nc.vector.tensor_tensor(eq[:], logits[:], best[:].unsqueeze(2).broadcast_to([P, TILES, EXP]), ALU.is_equal))
            r(nc.vector.memset(left[:], 1.0))
            for e in range(EXP - 1):
                r(nc.vector.tensor_tensor(oh[:, :, e], eq[:, :, e], left[:], ALU.mult))
                r(nc.vector.tensor_tensor(left[:], left[:], oh[:, :, e], ALU.subtract))
            r(nc.vector.tensor_copy(oh[:, :, EXP - 1], left[:]))
            N_OH = n_r
            assert N_OH == ONEHOT_STEPS
            dve.wait_ge(counted, 1)
            r(nc.vector.tensor_copy(tot[:], W[1][:, 0:TILES * EXP].rearrange("p (t e) -> p t e", e=EXP)))
            r(nc.vector.memset(base[:, 0, :], 0.0))
            for t in range(TILES):
                r(nc.vector.tensor_tensor(base[:, t + 1, :], base[:, t, :], tot[:, t, :], ALU.add))
            r(nc.vector.tensor_scalar(cnt_i[:], base[:, TILES, :], float(P - 1), None, ALU.add))
            r(nc.vector.tensor_scalar(cnt_s[:], cnt_i[:], 7, None, ALU.arith_shift_right))
            r(nc.vector.tensor_copy(cnt_f[:], cnt_s[:]))
            r(nc.vector.memset(end[:, 0:1], 0.0))
            for e in range(EXP):
                r(nc.vector.tensor_tensor(end[:, e + 1:e + 2], end[:, e:e + 1], cnt_f[:, e:e + 1], ALU.add))
            r(nc.vector.tensor_scalar(off[:], end[:, 0:EXP], float(P), None, ALU.mult))
            r(nc.vector.tensor_tensor(rank[:], base[:, 0:TILES, :], W[0][:, 0:TILES * EXP].rearrange("p (t e) -> p t e", e=EXP), ALU.add))
            r(nc.vector.tensor_tensor(rank[:], rank[:], off[:].unsqueeze(1).broadcast_to([P, TILES, EXP]), ALU.add))
            r(nc.vector.tensor_tensor(rank[:], rank[:], oh[:], ALU.mult))
            r(nc.vector.tensor_reduce(posf[:], rank[:], AX.X, ALU.add))
            nc.vector.tensor_copy(pos_i[:], posf[:]).then_inc(pos_ready, 1)
            dve.wait_ge(tile_num, 1)
            r(nc.vector.tensor_copy(tnum[:], tnum_i[:]))
            r(nc.vector.tensor_scalar(ecmp[:], tnum[:], end[:, 1:2], None, ALU.is_ge))
            for e in range(1, EXP - 1):
                r(nc.vector.scalar_tensor_tensor(out=ecmp[:], in0=tnum[:], scalar=end[:, e + 1:e + 2], in1=ecmp[:],
                                                 op0=ALU.is_ge, op1=ALU.add))
            r(nc.vector.tensor_copy(expert_i[:], ecmp[:]))
            assert n_r == ROUTE_STEPS

            n_f = 0

            def f(ins):
                nonlocal n_f
                n_f += 1
                ins.then_inc(f_self, 1)
                dve.wait_ge(f_self, n_f)

            for n in range(EXP * CH):
                dve.wait_ge(whi_ready, n + 1)
                nc.vector.tensor_tensor(wlo[:, n // CH, n % CH, :], raw[:, n % 2, :],
                                        whi[:, n // CH, n % CH, :].bitcast(F32), ALU.subtract).then_inc(wlo_ready, 1)

            def norm_rows(n):
                src = xs[:, n % XS, 0:DIM]
                dve.wait_ge(xs_in[n % XS], 16 * (n // XS + 1))
                f(nc.vector.bn_stats(fst[:], src))
                f(nc.vector.bn_aggr(fmv[:], fst[:]))
                nc.vector.tensor_scalar(fri[:], fmv[:, 1:2], EPS, None, ALU.add).then_inc(f_step, 1)
                dve.wait_ge(f_root, n + 1)
                if n >= 1:
                    dve.wait_ge(f_turn, n)
                nc.vector.tensor_scalar(fz[:], src, fmv[:, 0:1], frs[:], ALU.subtract, ALU.mult).then_inc(fz_ready, 1)

            def rows_low(n):
                dve.wait_ge(fzh_ready, n + 1)
                nc.vector.tensor_tensor(fzl[:].rearrange("p c n -> p (c n)"), W[0][:, 0:DIM],
                                        fzh[:].rearrange("p c n -> p (c n)").bitcast(F32), ALU.subtract)\
                    .then_inc(fzT_ready, 1)

            def add_rows(n):
                dve.wait_ge(down_ready, n + 1)
                if n >= 2:
                    dve.wait_ge(stored[n % 2], 16 * (n // 2))
                nc.vector.tensor_tensor(res[:, n % 2, :], xs[:, n % XS, 0:DIM], W[1][:, 0:DIM], ALU.add)\
                    .then_inc(res_ready, 1)

            norm_rows(0)
            rows_low(0)
            for n in range(SORTED):
                if n + 1 < SORTED:
                    norm_rows(n + 1)
                for c in range(2):
                    dve.wait_ge(gate_ready, 2 * n + c + 1)
                    dve.wait_ge(up_ready, 2 * n + 2)
                    nc.vector.tensor_tensor(gate[:, n % 2, c * 512:(c + 1) * 512], gate[:, n % 2, c * 512:(c + 1) * 512],
                                            O[c][:], ALU.mult).then_inc(h_ready, 1)
                if n + 1 < SORTED:
                    rows_low(n + 1)
                if n >= 1:
                    add_rows(n - 1)
            add_rows(SORTED - 1)

        @block.tensor
        def _(pe):
            pe.wait_ge(wk_in, 16 * 6)
            pe.wait_ge(consts, 14)
            for job, s in enumerate(setup):
                freed_wait(pe, job)
                w = W[job % WB]
                if s[0] == "kv":
                    m = s[1]
                    wt = wk if m < CH else wv
                    for c in range(CH):
                        mm = nc.tensor.matmul(w[:, 0:BATCH * CTX], wt[:, c, (m % CH) * P:(m % CH + 1) * P], ctxs[:, c, :],
                                              start=c == 0, stop=c == CH - 1)
                elif s[0] == "g":
                    _, b, c, n = s
                    pe.wait_ge(bd_ready, 2 + 4 * (b + 1))
                    mm = nc.tensor.matmul(w[:, 0:SB], wq2[:, n // 2, c * P:(c + 1) * P],
                                          kbd[:, n // 2, 4 * (n % 2):4 * (n % 2) + 4, :].rearrange("p h k -> p (h k)"),
                                          start=True, stop=True)
                elif s[0] == "bias":
                    _, b, n = s
                    mm = nc.tensor.matmul(w[:, 0:SB], bqb[:, n // 2, :],
                                          kbd[:, n // 2, 4 * (n % 2):4 * (n % 2) + 4, :].rearrange("p h k -> p (h k)"),
                                          start=True, stop=True)
                else:
                    _, b, n = s
                    m, cc = n // 5, n % 5
                    mm = nc.tensor.matmul(w[:, 0:DIM], vbd[:, m].rearrange("p h k -> p (h k)")[:, cc * P:(cc + 1) * P],
                                          wo2[:, m, :], start=True, stop=True)
                mm.then_inc(side_ready, 1)
            pe.wait_ge(wq_scaled, CH)
            pe.wait_ge(wo_in, 16)
            pe.wait_ge(dconst, 7)
            pe.wait_ge(bias_step, 5 * BATCH + 1)

            def scores_of(k):
                t, g, j = steps[k]
                if k >= AHEAD:
                    pe.wait_ge(p_ready, k - AHEAD + 1)
                if g == 0 and j == 0:
                    pe.wait_ge(act_freed, freed_count("q_turn", 4, t))
                    pe.wait_ge(dve_freed, freed_count("q_turn", 3, t))
                ks = (t - t % TPB + j) % KV
                q = qT[t % 2][:, HPG * g:HPG * (g + 1), :].rearrange("p h q -> p (h q)")
                nc.tensor.matmul(S[k % AHEAD][:], kT[:, ks, 0, :], q, start=True, stop=False)
                nc.tensor.matmul(S[k % AHEAD][:], kT[:, ks, 1, :], q, start=False, stop=True).then_inc(s_ready, 1)

            def values_of(k):
                t, g, j = steps[k]
                G_ = GROUPS * t + g
                o = O[G_ % 2][0:DH + 1, :]
                if j == 0:
                    if G_ >= 2:
                        pe.wait_ge(ot_ready, G_ - 1)
                    if g == 0:
                        pe.wait_ge(v_ready, 2 * (t + 1))
                vs = (t - t % TPB + j) % KV
                last = j == t % TPB
                pe.wait_ge(ph_ready, k + 1)
                nc.tensor.matmul(o, vhi[:, vs, 0:DH + 1], ph[:, k % RING, :], start=j == 0, stop=False)
                nc.tensor.matmul(o, vlo[:, vs, 0:DH + 1], ph[:, k % RING, :], start=False, stop=False)
                pe.wait_ge(pl_ready, k + 1)
                nc.tensor.matmul(o, vhi[:, vs, 0:DH + 1], pl[:, k % RING, :], start=False, stop=last).then_inc(pv_done, 1)

            for k, stages in program("pe"):
                if k == 0:
                    for n in range(AHEAD):
                        scores_of(n)
                if k is not None:
                    values_of(k)
                    if k + AHEAD < N_STEPS:
                        scores_of(k + AHEAD)
                for name, part, t, job in stages:
                    b = t // TPB
                    if name == "z_turn":
                        pe.wait_ge(z_ready, t + 1)
                        freed_wait(pe, job)
                        for c in range(CH):
                            mm = nc.tensor.transpose(W[job % WB][:, c * P:(c + 1) * P], z[t % 2][:, c * P:(c + 1) * P], ident[:])
                        mm.then_inc(side_ready, 1)
                    elif name == "qkv":
                        pe.wait_ge(act_freed, freed_count("z_turn", 0, t))
                        freed_wait(pe, job)
                        for c in range(CH):
                            mm = nc.tensor.matmul(W[job % WB][:, 0:QB], zT[:, c, :], wqkv[:, c, part * QB:(part + 1) * QB],
                                                  start=c == 0, stop=c == CH - 1)
                        mm.then_inc(side_ready, 1)
                    elif name == "q_turn":
                        pe.wait_ge(qlo_ready, t + 1)
                        pe.wait_ge(kdup_ready, 2 * (t + 1))
                        freed_wait(pe, job)
                        for h in range(4 if part < 4 else 2):
                            src = qhl[:, 4 * part + h].bitcast(F32) if part < 4 else kdup[:, h]
                            mm = nc.tensor.transpose(W[job % WB][:, h * P:(h + 1) * P], src.rearrange("p a d -> p (a d)"),
                                                     ident[:])
                        mm.then_inc(side_ready, 1)
                    elif name == "heads_out":
                        pe.wait_ge(ot_ready, GROUPS * t + part + 1)
                        freed_wait(pe, job)
                        for h in range(HPG):
                            mm = nc.tensor.transpose(W[job % WB][:, h * (DH + 1):(h + 1) * (DH + 1)],
                                                     oT[0:DH + 1, (GROUPS * t + part) % 2, h * P:(h + 1) * P],
                                                     ident[0:DH + 1, 0:DH + 1])
                        mm.then_inc(side_ready, 1)
                    elif name == "out_turn":
                        pe.wait_ge(dve_freed, freed_count("heads_out", 3, t))
                        freed_wait(pe, job)
                        for c in range(4):
                            mm = nc.tensor.transpose(W[job % WB][:, c * P:(c + 1) * P],
                                                     on[t % 2][:, (4 * part + c) * P:(4 * part + c + 1) * P], ident[:])
                        mm.then_inc(side_ready, 1)
                    elif name == "out_proj":
                        pe.wait_ge(act_freed, freed_count("out_turn", 1, t))
                        freed_wait(pe, job)
                        for c in range(8):
                            mm = nc.tensor.matmul(W[job % WB][:, 0:DIM], onT[:, c, :], wout[:, c, :], start=c == 0, stop=c == 7)
                        mm.then_inc(side_ready, 1)
                    elif name == "z2_turn":
                        pe.wait_ge(z2_ready, t + 1)
                        freed_wait(pe, job)
                        for c in range(CH):
                            mm = nc.tensor.transpose(W[job % WB][:, c * P:(c + 1) * P], z2[:, c * P:(c + 1) * P], ident[:])
                        mm.then_inc(side_ready, 1)
                    elif name == "scores":
                        pe.wait_ge(act_freed, freed_count("z2_turn", 0, t))
                        freed_wait(pe, job)
                        w = W[job % WB][:, 0:SB]
                        nc.tensor.matmul(w, pick[:], BI[b][:, part * SB:(part + 1) * SB], start=True, stop=False)
                        for c in range(CH):
                            mm = nc.tensor.matmul(w, z2T[:, c, :], G[b][:, c, part * SB:(part + 1) * SB],
                                                  start=False, stop=c == CH - 1)
                        mm.then_inc(side_ready, 1)
                    elif name == "probs_turn":
                        pe.wait_ge(pn_ready, t + 1)
                        pn = sc[:].rearrange("p h k -> p (h k)")
                        freed_wait(pe, job)
                        for c in range(4 * part, min(4 * part + 4, HKC)):
                            mm = nc.tensor.transpose(W[job % WB][:, (c - 4 * part) * P:(c - 4 * part + 1) * P],
                                                     pn[:, c * P:(c + 1) * P], ident[:])
                        mm.then_inc(side_ready, 1)
                    elif name == "xattn_out":
                        pe.wait_ge(act_freed, freed_count("probs_turn", 2, t))
                        pe.wait_ge(dve_freed, freed_count("probs_turn", 1, t))
                        freed_wait(pe, job)
                        for c in range(HKC):
                            mm = nc.tensor.matmul(W[job % WB][:, 0:DIM], pT[:, c, :], VP[b][:, c, :], start=c == 0, stop=c == HKC - 1)
                        mm.then_inc(side_ready, 1)
            pe.wait_ge(side_ready, N_SIDE)
            pe.sem_inc(pe_done, 1)

            pe.wait_ge(route, ONEHOT_STEPS)
            oh2 = oh[:].rearrange("p t e -> p (t e)")
            nc.tensor.matmul(W[0][:, 0:TILES * EXP], tri[:], oh2, start=True, stop=True)
            nc.tensor.matmul(W[1][:, 0:TILES * EXP], ones[:], oh2, start=True, stop=True).then_inc(counted, 1)
            pe.wait_ge(route, ROUTE_STEPS)
            pe.wait_ge(ffn_w, 16 * EXP)
            pe.wait_ge(wlo_ready, EXP * CH)

            def turn_rows(n):
                pe.wait_ge(fz_ready, n + 1)
                if n >= 1:
                    pe.wait_ge(fzT_ready, n)
                for c in range(CH):
                    mm = nc.tensor.transpose(W[0][:, c * P:(c + 1) * P], fz[:, c * P:(c + 1) * P], ident[:])
                mm.then_inc(f_turn, 1)

            def up(n):
                expert = pe.value_load(expert_i[0:1, n:n + 1], min_val=0, max_val=EXP - 1)
                pe.wait_ge(fzT_ready, n + 1)
                hi, lo = (w[:].rearrange("p e c n -> p (e c n)") for w in (whi, wlo))
                passes = [(rows, w, c) for c in range(CH) for rows, w in ((fzh, hi), (fzl, hi), (fzh, lo))]
                for part, banks in ((0, S[0:2]), (1, O)):
                    for q in range(2):
                        if n >= 1:
                            pe.wait_ge(gate_ready if part == 0 else h_ready, 2 * (n - 1) + q + 1)
                        for m, (rows, w, c) in enumerate(passes):
                            at = expert * (CH * 2 * HID) + (c * 2 * HID + part * HID + q * 512)
                            mm = nc.tensor.matmul(banks[q][:], rows[:, c, :], w[:, bass.ds(at, 512)],
                                                  start=m == 0, stop=m == len(passes) - 1)
                    mm.then_inc(up_ready, 1)
                return expert

            def turn_hidden(n):
                pe.wait_ge(h_ready, 2 * n + 2)
                for q in range(2):
                    if n >= 1:
                        pe.wait_ge(hT_ready, 2 * (n - 1) + q + 1)
                    for c in range(4):
                        mm = nc.tensor.transpose(HT[q][:, c * P:(c + 1) * P],
                                                 gate[:, n % 2, (4 * q + c) * P:(4 * q + c + 1) * P], ident[:])
                    mm.then_inc(h_turned, 1)

            def down(n, expert):
                if n >= 1:
                    pe.wait_ge(res_ready, n)
                flat = wps[:].rearrange("p e c n -> p (e c n)")
                for c in range(HID // P):
                    if c % 4 == 0:
                        pe.wait_ge(hT_ready, 2 * n + c // 4 + 1)
                    at = expert * (HID // P * DIM) + c * DIM
                    mm = nc.tensor.matmul(W[1][:, 0:DIM], hT[:, c, :], flat[:, bass.ds(at, DIM)],
                                          start=c == 0, stop=c == HID // P - 1)
                mm.then_inc(down_ready, 1)

            turn_rows(0)
            before = None
            for n in range(SORTED):
                expert = up(n)
                if n + 1 < SORTED:
                    turn_rows(n + 1)
                if n >= 1:
                    turn_hidden(n - 1)
                    down(n - 1, before)
                before = expert
            turn_hidden(SORTED - 1)
            down(SORTED - 1, before)



ONEHOT_STEPS = 10
ROUTE_STEPS = 46


def kernel(**inputs):
    import numpy as np
    import concourse.bacc as bacc
    from concourse.bass_utils import run_bass_kernel_spmd

    i = {k: np.asarray(v) for k, v in inputs.items()}
    wqkv = np.concatenate([i["L0_attn_Wq"], i["L0_attn_Wkv"]], axis=0)
    arrays = {
        "x": i["x"].reshape(TOKENS, DIM),
        "wqkv_t": wqkv.T,
        "wout_t": i["L0_attn_Wout"].T,
        "g1": i["L0_attn_g1"].reshape(CH, P).T,
        "g2": i["L0_attn_g2"],
        "ctx_t": i["ctx_1024"].transpose(2, 0, 1).reshape(DIM, BATCH * CTX),
        "xwq": i["L0_xattn_W_q"],
        "xwk_t": i["L0_xattn_W_k"].T,
        "xwv_t": i["L0_xattn_W_v"].T,
        "xwout_t": i["L0_xattn_W_out"].T,
        "biases": np.stack([i[f"L0_xattn_b_{w}"].reshape(CH, P).T for w in "qkv"], axis=1),
        "xbout": i["L0_xattn_b_out"],
        "wr_t": i["L0_ffn_w_router"].T,
        "w_v": i["L0_ffn_w_v"],
        "w_proj": i["L0_ffn_w_proj"],
    }
    nc = bacc.Bacc("TRN2", target_bir_lowering=False, num_devices=1)
    args, feed = {}, {}
    for name, a in arrays.items():
        a = np.ascontiguousarray(a)
        feed[f"in_{name}"] = a
        args[name] = nc.dram_tensor(f"in_{name}", a.shape, mybir.dt.from_np(a.dtype), kind="ExternalInput").ap()
    out = nc.dram_tensor("out_0", (TOKENS, DIM), F32, kind="ExternalOutput").ap()
    build(nc, out=out, **args)
    r = run_bass_kernel_spmd(nc, [feed], core_ids=[0])
    return r.results[0]["out_0"].reshape(BATCH, SEQ, DIM)
```
